# Optimizing a Trainium2 kernel written in Bass

```python
import numpy as np
import jax
import jax.numpy as jnp

def _softmax(x, axis=-1):
    return jax.nn.softmax(x, axis=axis)

def _gelu(x):
    return jax.nn.gelu(x, approximate=True)

def _silu(x):
    return jax.nn.silu(x)

def _sigmoid(x):
    return jax.nn.sigmoid(x)

def _layernorm(x, axis=-1, eps=1e-05):
    m = jnp.mean(x, axis=axis, keepdims=True)
    v = jnp.var(x, axis=axis, keepdims=True)
    return (x - m) / jnp.sqrt(v + eps)

def _scatter_add(tgt, idx, src, axis=0):
    return tgt.at[idx].add(src)

def _segment_sum(src, seg, n):
    return jax.ops.segment_sum(src, seg, n)
kernel_name = 'mk_xattn_seq_d1_seqx_r4_890192'

def setup_inputs(seed: int=0):
    np.random.seed(seed)
    _w = jnp.asarray

    def _rec_inputs():
        import jax
        import jax.numpy as jnp
        _rk = jax.random.key(seed)
        x = -0.0002928 + 1 * jax.random.normal(jax.random.fold_in(_rk, 1), (4, 1024, 256), jnp.float32)
        _lenS = 1024 - jax.random.randint(jax.random.fold_in(_rk, 7), (4,), 0, max(1, 1024 // 4) + 1, jnp.int32)
        _lenS2 = 64 - jax.random.randint(jax.random.fold_in(_rk, 8), (4,), 0, max(1, 64 // 4) + 1, jnp.int32)
        _ctx_768P = jax.random.normal(jax.random.fold_in(_rk, 11), (4, 16, 192), jnp.float32)
        _ctx_768c = jax.random.dirichlet(jax.random.fold_in(_rk, 511), 0.3 * jnp.ones((16,), jnp.float32), (4, 64))
        _ctx_768t = jnp.einsum('bsk,bkd->bsd', _ctx_768c, _ctx_768P)
        _ctx_768t = _ctx_768t * jax.lax.rsqrt(jnp.mean(jnp.square(_ctx_768t)) + 1e-12) * 0.953939
        ctx_768 = -0.00423632 + 0.9977 * (_ctx_768t + 0.3 * jax.random.normal(jax.random.fold_in(_rk, 611), (4, 64, 192), jnp.float32))
        return (x, ctx_768)
    x, ctx_768 = _rec_inputs()

    def _L0_xattn_setup():
        import jax, jax.numpy as jnp
        import numpy as np
        DIM, HEADS, DHEAD, CTX_DIM = (256, 16, 64, 192)
        INNER = HEADS * DHEAD
        FF_HID = 4 * DIM
        EPS = 1e-05

        def _ln(x, g, b):
            mu = jnp.mean(x, axis=-1, keepdims=True)
            var = jnp.mean(jnp.square(x - mu), axis=-1, keepdims=True)
            return (x - mu) * jax.lax.rsqrt(var + EPS) * g + b

        def _attn(x, ctx, Wq, Wk, Wv, Wo, bo):
            b, n, _ = x.shape
            m = ctx.shape[1]
            q = (x @ Wq).reshape(b, n, HEADS, DHEAD)
            k = (ctx @ Wk).reshape(b, m, HEADS, DHEAD)
            v = (ctx @ Wv).reshape(b, m, HEADS, DHEAD)
            scale = DHEAD ** (-0.5)
            sim = jnp.einsum('bihd,bjhd->bhij', q, k) * scale
            attn = jax.nn.softmax(sim, axis=-1)
            out = jnp.einsum('bhij,bjhd->bihd', attn, v).reshape(b, n, INNER)
            return out @ Wo + bo
        key = jax.random.key(seed)
        ks = jax.random.split(key, 24)

        def w(k, shape, fan_in):
            return jax.random.normal(k, shape, jnp.float32) * fan_in ** (-0.5)
        inp = {'x': jax.random.normal(ks[0], (2, 512, DIM), jnp.float32), 'context': jax.random.normal(ks[1], (2, 77, CTX_DIM), jnp.float32), 'Wq1': w(ks[2], (DIM, INNER), DIM), 'Wk1': w(ks[3], (DIM, INNER), DIM), 'Wv1': w(ks[4], (DIM, INNER), DIM), 'Wo1': w(ks[5], (INNER, DIM), INNER), 'bo1': jnp.zeros((DIM,), jnp.float32), 'Wq2': w(ks[6], (DIM, INNER), DIM), 'Wk2': w(ks[7], (CTX_DIM, INNER), CTX_DIM), 'Wv2': w(ks[8], (CTX_DIM, INNER), CTX_DIM), 'Wo2': w(ks[9], (INNER, DIM), INNER), 'bo2': jnp.zeros((DIM,), jnp.float32), 'Wp': w(ks[10], (DIM, 2 * FF_HID), DIM), 'bp': jnp.zeros((2 * FF_HID,), jnp.float32), 'W2': w(ks[11], (FF_HID, DIM), FF_HID), 'b2': jnp.zeros((DIM,), jnp.float32), 'g1': jnp.ones((DIM,), jnp.float32), 'be1': jnp.zeros((DIM,), jnp.float32), 'g2': jnp.ones((DIM,), jnp.float32), 'be2': jnp.zeros((DIM,), jnp.float32), 'g3': jnp.ones((DIM,), jnp.float32), 'be3': jnp.zeros((DIM,), jnp.float32)}
        return inp
    _L0_xattn_all = _L0_xattn_setup()
    _L0_xattn_in = {k: v for k, v in _L0_xattn_all.items() if k in ('Wq1', 'Wk1', 'Wv1', 'Wo1', 'bo1', 'Wq2', 'Wk2', 'Wv2', 'Wo2', 'bo2', 'Wp', 'bp', 'W2', 'b2', 'g1', 'be1', 'g2', 'be2', 'g3', 'be3')}
    del _L0_xattn_all
    return {'x': x, 'ctx_768': ctx_768, 'L0_xattn_Wq1': _L0_xattn_in['Wq1'], 'L0_xattn_Wk1': _L0_xattn_in['Wk1'], 'L0_xattn_Wv1': _L0_xattn_in['Wv1'], 'L0_xattn_Wo1': _L0_xattn_in['Wo1'], 'L0_xattn_bo1': _L0_xattn_in['bo1'], 'L0_xattn_Wq2': _L0_xattn_in['Wq2'], 'L0_xattn_Wk2': _L0_xattn_in['Wk2'], 'L0_xattn_Wv2': _L0_xattn_in['Wv2'], 'L0_xattn_Wo2': _L0_xattn_in['Wo2'], 'L0_xattn_bo2': _L0_xattn_in['bo2'], 'L0_xattn_Wp': _L0_xattn_in['Wp'], 'L0_xattn_bp': _L0_xattn_in['bp'], 'L0_xattn_W2': _L0_xattn_in['W2'], 'L0_xattn_b2': _L0_xattn_in['b2'], 'L0_xattn_g1': _L0_xattn_in['g1'], 'L0_xattn_be1': _L0_xattn_in['be1'], 'L0_xattn_g2': _L0_xattn_in['g2'], 'L0_xattn_be2': _L0_xattn_in['be2'], 'L0_xattn_g3': _L0_xattn_in['g3'], 'L0_xattn_be3': _L0_xattn_in['be3']}

def reference(x, ctx_768, L0_xattn_Wq1, L0_xattn_Wk1, L0_xattn_Wv1, L0_xattn_Wo1, L0_xattn_bo1, L0_xattn_Wq2, L0_xattn_Wk2, L0_xattn_Wv2, L0_xattn_Wo2, L0_xattn_bo2, L0_xattn_Wp, L0_xattn_bp, L0_xattn_W2, L0_xattn_b2, L0_xattn_g1, L0_xattn_be1, L0_xattn_g2, L0_xattn_be2, L0_xattn_g3, L0_xattn_be3):
    import jax
    import jax.numpy as jnp

    def _L0_xattn_ref(x, context, Wq1, Wk1, Wv1, Wo1, bo1, Wq2, Wk2, Wv2, Wo2, bo2, Wp, bp, W2, b2, g1, be1, g2, be2, g3, be3):
        import jax, jax.numpy as jnp
        import numpy as np
        DIM, HEADS, DHEAD, CTX_DIM = (256, 16, 64, 192)
        INNER = HEADS * DHEAD
        FF_HID = 4 * DIM
        EPS = 1e-05

        def _ln(x, g, b):
            mu = jnp.mean(x, axis=-1, keepdims=True)
            var = jnp.mean(jnp.square(x - mu), axis=-1, keepdims=True)
            return (x - mu) * jax.lax.rsqrt(var + EPS) * g + b

        def _attn(x, ctx, Wq, Wk, Wv, Wo, bo):
            b, n, _ = x.shape
            m = ctx.shape[1]
            q = (x @ Wq).reshape(b, n, HEADS, DHEAD)
            k = (ctx @ Wk).reshape(b, m, HEADS, DHEAD)
            v = (ctx @ Wv).reshape(b, m, HEADS, DHEAD)
            scale = DHEAD ** (-0.5)
            sim = jnp.einsum('bihd,bjhd->bhij', q, k) * scale
            attn = jax.nn.softmax(sim, axis=-1)
            out = jnp.einsum('bhij,bjhd->bihd', attn, v).reshape(b, n, INNER)
            return out @ Wo + bo
        h = _ln(x, g1, be1)
        x = _attn(h, h, Wq1, Wk1, Wv1, Wo1, bo1) + x
        h = _ln(x, g2, be2)
        x = _attn(h, context, Wq2, Wk2, Wv2, Wo2, bo2) + x
        h = _ln(x, g3, be3)
        y = h @ Wp + bp
        a, gate = (y[..., :FF_HID], y[..., FF_HID:])
        x = a * jax.nn.gelu(gate, approximate=False) @ W2 + b2 + x
        return x
    x = _L0_xattn_ref(x, ctx_768, L0_xattn_Wq1, L0_xattn_Wk1, L0_xattn_Wv1, L0_xattn_Wo1, L0_xattn_bo1, L0_xattn_Wq2, L0_xattn_Wk2, L0_xattn_Wv2, L0_xattn_Wo2, L0_xattn_bo2, L0_xattn_Wp, L0_xattn_bp, L0_xattn_W2, L0_xattn_b2, L0_xattn_g1, L0_xattn_be1, L0_xattn_g2, L0_xattn_be2, L0_xattn_g3, L0_xattn_be3)
    return x

_drawn_inputs = setup_inputs


def setup_inputs(seed=0):
    import zlib

    import numpy as np

    out = dict(_drawn_inputs(seed))
    spreads = {'L0_xattn_bo1': (0.0, 0.1),
     'L0_xattn_bo2': (0.0, 0.1),
     'L0_xattn_bp': (0.0, 0.1),
     'L0_xattn_b2': (0.0, 0.1),
     'L0_xattn_g1': (1.0, 0.2),
     'L0_xattn_be1': (0.0, 0.1),
     'L0_xattn_g2': (1.0, 0.2),
     'L0_xattn_be2': (0.0, 0.329),
     'L0_xattn_g3': (1.0, 0.2),
     'L0_xattn_be3': (0.0, 0.1)}
    factors = {}
    for name, (base, spread) in spreads.items():
        noise = np.random.default_rng([zlib.crc32(name.encode()), seed]).standard_normal(out[name].shape)
        drawn = base * np.exp(spread * noise) if base else spread * noise
        out[name] = jnp.asarray(drawn.astype(out[name].dtype))
    for name, factor in factors.items():
        out[name] = (out[name] * factor).astype(out[name].dtype)
    return out
```

```python
from contextlib import ExitStack

import concourse.bass as bass
from concourse import mybir
from concourse.alu_op_type import AluOpType as ALU

F32 = mybir.dt.float32
F32R = mybir.dt.float32r
ACT = mybir.ActivationFunctionType
AX = mybir.AxisListType

PART = 128
BANK = 512
EPS = 1e-5


class Queues:

    def __init__(self, semaphore):
        self.semaphore = semaphore
        self.streams = {"tensor": [], "vector": [], "scalar": [], "gpsimd": [], "sync": []}
        self.raised = {}

    def put(self, engine, emit, waits=(), signal=None, step=1):
        ticket = None
        if signal is not None:
            self.raised[signal] = self.raised.get(signal, 0) + step
            ticket = (signal, self.raised[signal])
        self.streams[engine].append((emit, waits, signal, step))
        return ticket

    def dma(self, emit, waits=(), signal=None):
        return self.put("sync", emit, waits, signal, 16)

    def play(self, name, engine):
        seen = {}
        for emit, waits, signal, step in self.streams[name]:
            for ticket in waits:
                if ticket is not None and seen.get(ticket[0], 0) < ticket[1]:
                    engine.wait_ge(self.semaphore(ticket[0]), ticket[1])
                    seen[ticket[0]] = ticket[1]
            last = emit(engine)
            if signal is not None:
                last.then_inc(self.semaphore(signal), step)


def block_kernel(nc, x, ctx, Wq1, Wk1, Wv1, Wo1, bo1, Wq2, Wk2, Wv2, Wo2, bo2, Wp, bp, W2, b2,
                 g1, be1, g2, be2, g3, be3, out):
    B, N, DIM = x.shape
    M, CD = ctx.shape[1:]
    INNER = Wq1.shape[1]
    DH = 64
    HEADS = INNER // DH
    SCALE = DH ** -0.5
    FF = W2.shape[0]
    KT = DIM // PART
    PAIRS = HEADS // 2
    TILES = N // PART
    CHUNKS = N // BANK
    TPC = BANK // PART
    FT = FF // PART
    CREST = CD - PART

    stack = ExitStack()
    with stack:
        def sb(name, shape, dt=F32):
            return stack.enter_context(nc.sbuf_tensor(name, shape, dt))

        def ps(name, shape):
            return stack.enter_context(nc.psum_tensor(name, shape, F32))

        ident = sb("ident", [PART, PART])
        eps = sb("eps", [PART, 1])
        cols = sb("cols", [PART, 6, KT])
        bp_col = sb("bp_col", [PART, 2 * FT])
        rows = sb("rows", [PART, 3, DIM])
        wo1 = sb("wo1", [PART, PAIRS, DIM])
        wq2 = sb("wq2", [PART, KT, INNER])
        wo2 = sb("wo2", [PART, PAIRS, DIM])
        wqkv = sb("wqkv", [PART, 2, 3, KT, PART])
        cross = sb("cross", [PART, 2, PAIRS, PART])
        xres = sb("xres", [PART, 2, TILES, DIM])
        hT = sb("hT", [PART, KT, N])
        xn = sb("xn", [PART, 4, DIM])
        stats = sb("stats", [PART, TILES, 6])
        mv = sb("mv", [PART, TILES, 2])
        mv3 = sb("mv3", [PART, B, TILES, 2])
        sd = sb("sd", [PART, B * TILES])
        rs = sb("rs", [PART, B * TILES])
        v_sb = sb("v_sb", [PART, 2, TILES, PART])
        with nc.sbuf_tensor("qk", [PART, 2, 2, 3, N], F32R) as qk:
            pass
        wide = sb("wide", [PART, 2 * 2 * 3 * N])
        probs = sb("probs", [PART, 3, N])
        pT = sb("pT", [PART, 2, 2, TILES, 2 * PART])
        oT = sb("oT", [PART, PAIRS, N])
        nmax = sb("nmax", [PART, 8])
        lsum = sb("lsum", [PART, 8])
        rsum = sb("rsum", [PART, 8])
        nmax2 = sb("nmax2", [PART, 2, HEADS])
        lsum2 = sb("lsum2", [PART, 2, HEADS])
        rsum2 = sb("rsum2", [PART, 2, HEADS])

        SC = [ps(f"score{i}", [PART, 2 * BANK]) for i in range(2)]
        TP = [ps(f"turn{i}", [PART, BANK]) for i in range(2)]
        PV = ps("attn_out", [PART, BANK])
        PJ = ps("project", [PART, BANK])
        banks = {"S0a": SC[0][:, 0:BANK], "S0b": SC[0][:, BANK:], "S1a": SC[1][:, 0:BANK],
                 "S1b": SC[1][:, BANK:], "T0": TP[0][:, :], "T1": TP[1][:, :], "PV": PV[:, :], "PJ": PJ[:, :]}
        freed = {name: None for name in banks}

        oflat = oT[:, :, :].rearrange("p a n -> p (a n)")
        wk2 = oflat[:, 0:2 * INNER].rearrange("p (k n) -> p k n", k=2)
        wv2 = oflat[:, 2 * INNER:4 * INNER].rearrange("p (k n) -> p k n", k=2)
        o0 = 4 * INNER
        ctxT = oflat[:, o0:o0 + 2 * B * 2 * M].rearrange("p (k b t m) -> p k b t m", k=2, b=B, t=2)
        o0 += 2 * B * 2 * M
        ctx_sb = oflat[:, o0:o0 + 2 * CD].rearrange("p (a c) -> p a c", a=2)
        stage = pT[:, :, :, :, :].rearrange("p a h t n -> p (a h t n)").rearrange(
            "p (b w q n) -> p b w q n", b=B, w=2, q=PAIRS)
        q2T = oT
        qkflat = wide[:, :]
        p2T = qkflat[:, 0:2 * PAIRS * BANK].rearrange("p (c q n) -> p c q n", c=2, q=PAIRS)
        o2T = qkflat[:, 2 * PAIRS * BANK:3 * PAIRS * BANK].rearrange("p (q n) -> p q n", q=PAIRS)
        ptflat = pT[:, :, :, :, :].rearrange("p a h t n -> p (a h t n)")
        wp = ptflat[:, 0:KT * 2 * FF].rearrange("p (k n) -> p k n", k=KT)
        w2 = ptflat[:, KT * 2 * FF:KT * 2 * FF + FT * DIM].rearrange("p (f n) -> p f n", f=FT)
        uT = qkflat[:, 0:2 * FT * BANK].rearrange("p (c f n) -> p c f n", c=2, f=FT)
        xf = oflat[:, 0:3 * TPC * DIM].rearrange("p (c t n) -> p c t n", c=3, t=TPC)
        o0 = 3 * TPC * DIM
        gate = oflat[:, o0:o0 + 3 * BANK].rearrange("p (g n) -> p g n", g=3)
        o0 += 3 * BANK
        yf = oflat[:, o0:o0 + 2 * TPC * DIM].rearrange("p (c t n) -> p c t n", c=2, t=TPC)

        cross_dram = nc.dram_tensor("cross_tiles", (B, PART, 2 * PAIRS * PART), F32, kind="Internal").ap()
        xmid = nc.dram_tensor("x_middle", (B, PART, TILES, DIM), F32, kind="Internal").ap()

        sems = {}

        def semaphore(name):
            if name not in sems:
                sems[name] = stack.enter_context(nc.semaphore(name))
            return sems[name]

        Q = Queues(semaphore)
        put, dma = Q.put, Q.dma

        def load_x(b, waits=()):
            return dma(lambda e: e.dma_start(xres[:, b % 2], x[b].rearrange("(t p) d -> p t d", p=PART)),
                       waits, f"x_loaded{b % 2}")

        x_in = {0: load_x(0)}
        for i, v in enumerate((g1, be1, g2, be2, g3, be3)):
            cols_in = dma(lambda e, i=i, v=v: e.dma_start(cols[:, i, :], v.rearrange("(k p) -> p k", p=PART), allow_slow_non_contiguous=True),
                          signal="cols_loaded")
        ctx_rows = ctx.rearrange("b m c -> (b m) c").rearrange("(a p) c -> p a c", p=PART)
        ctx_in = dma(lambda e: e.dma_start(ctx_sb, ctx_rows), signal="ctx_loaded")

        def load_wqkv(P, waits=()):
            p, t = P % PAIRS, None
            for i, w in enumerate((Wq1, Wk1, Wv1)):
                src = w.rearrange("(k p) n -> p k n", p=PART)[:, :, p * PART:(p + 1) * PART]
                t = dma(lambda e, i=i, src=src: e.dma_start(wqkv[:, P % 2, i], src), waits, f"wqkv_loaded{P % 2}")
            return t

        wqkv_in = {0: load_wqkv(0), 1: load_wqkv(1)}
        for w, dst in ((Wk2, wk2), (Wv2, wv2)):
            dma(lambda e, w=w, dst=dst: e.dma_start(dst[:, 0], w[0:PART]), signal="wkv2_loaded")
            wkv2_in = dma(lambda e, w=w, dst=dst: e.dma_start(dst[0:CREST, 1], w[PART:CD]), signal="wkv2_loaded")
        for i, v in enumerate((bo1, bo2, b2)):
            rows_in = dma(lambda e, i=i, v=v: e.dma_start(
                rows[:, i, :], v.rearrange("(a n) -> a n", a=1).to_broadcast([PART, DIM])), signal="rows_loaded")
        bp_in = dma(lambda e: e.dma_start(bp_col[:, :], bp.rearrange("(f p) -> p f", p=PART),
                                         allow_slow_non_contiguous=True), signal="bp_loaded")
        dma(lambda e: e.dma_start(wo1[:, :, :], Wo1.rearrange("(q p) n -> p q n", p=PART)), signal="w_loaded")
        dma(lambda e: e.dma_start(wq2[:, :, :], Wq2.rearrange("(k p) n -> p k n", p=PART)), signal="w_loaded")
        w_in = dma(lambda e: e.dma_start(wo2[:, :, :], Wo2.rearrange("(q p) n -> p q n", p=PART)),
                   signal="w_loaded")

        t = put("gpsimd", lambda e: e.memset(ident[:, :], 0.0), signal="const")
        ident_in = put("gpsimd", lambda e: e.affine_select(
            out=ident[:, :], in_=ident[:, :], compare_op=ALU.not_equal, fill=1.0, base=0,
            pattern=[[-1, PART]], channel_multiplier=1), (t,), "const")
        eps_in = put("gpsimd", lambda e: e.memset(eps[:, :], EPS), signal="const")
        stage_zero = put("gpsimd", lambda e: e.memset(ptflat, 0.0), signal="const")

        def ln_stats(tile_of, count, mv_of, first, waits):
            for t in range(count):
                st = put("vector", lambda e, t=t: e.bn_stats(stats[:, t, :], tile_of(t)), (waits[t], last_agg[0]), "ln_stat")
            for t in range(count):
                agg = put("vector", lambda e, t=t: e.bn_aggr(mv_of(t), stats[:, t, :]), (st,), "ln_stat")
            last_agg[0] = agg
            return agg

        def ln_rstd(var, first, count, waits):
            root = put("scalar", lambda e: e.activation(sd[:, first:first + count], var, ACT.Sqrt,
                                                        bias=eps[:, 0:1]), (*waits, eps_in), "ln_root")
            return put("vector", lambda e: e.reciprocal(rs[:, first:first + count], sd[:, first:first + count]),
                       (root,), "ln_stat")

        last_agg = [None]
        xn_read = {}
        xn_count = [0]

        def ln_rows(src, mean, r, waits):
            slot = xn_count[0] % 4
            xn_count[0] += 1
            t = put("vector", lambda e: e.tensor_scalar(xn[:, slot, :], src, mean, r, ALU.subtract, ALU.mult),
                    (*waits, xn_read.get(slot)), "ln_rows")
            return slot, t

        def ln_turn(c, slots, which, hT_free):
            done = []
            for k in range(KT):
                bank = f"T{k}"
                for j, (slot, ready) in enumerate(slots):
                    turned = put("tensor", lambda e, j=j, slot=slot, k=k, bank=bank: e.transpose(
                        banks[bank][:, j * PART:(j + 1) * PART], xn[:, slot, k * PART:(k + 1) * PART],
                        ident[:, :]), (ready, ident_in, freed[bank]), "ln_turned")
                    if k == KT - 1:
                        xn_read[slot] = turned
                g, b = cols[:, 2 * which, k:k + 1], cols[:, 2 * which + 1, k:k + 1]
                dst = hT[:, k, c * BANK:(c + 1) * BANK]
                if k % 2 == 0:
                    t = put("scalar", lambda e, g=g, b=b, dst=dst, bank=bank: e.activation(
                        dst, banks[bank], ACT.Identity, bias=b, scale=g), (turned, cols_in, hT_free), "hT_act")
                else:
                    t = put("vector", lambda e, g=g, b=b, dst=dst, bank=bank: e.tensor_scalar(
                        dst, banks[bank], g, b, ALU.mult, ALU.add), (turned, cols_in, hT_free), "hT_dve")
                freed[bank] = t
                done.append(t)
            return done

        def layer_norm(b, which, ready, first, hT_free):
            tile = lambda t: xres[:, b % 2, t, :]
            mvt = (lambda t: mv[:, t, :])
            agg = ln_stats(tile, TILES, mvt, first, ready)
            r = ln_rstd(mv[:, :, 1], first, TILES, (agg,))
            out_t = {}
            for c in range(CHUNKS):
                slots = [ln_rows(tile(t), mv[:, t, 0:1], rs[:, first + t:first + t + 1], (r,))
                         for t in range(c * TPC, (c + 1) * TPC)]
                out_t[c] = ln_turn(c, slots, which, hT_free)
            return out_t, slots[-1][1]

        def context():
            t = None
            for a in range(2):
                bpt = PART // M
                for k, rows_k in ((0, PART), (1, CREST)):
                    bank = f"T{k}"
                    t = put("tensor", lambda e, a=a, k=k, rows_k=rows_k, bank=bank: e.transpose(
                        banks[bank][0:rows_k, 0:PART], ctx_sb[:, a, k * PART:k * PART + rows_k], ident[:, :]),
                        (ctx_in, ident_in, freed[bank]), "ctx_turned")
                    for half in range(2):
                        t2 = put("vector", lambda e, a=a, k=k, rows_k=rows_k, bank=bank, half=half: e.tensor_copy(
                            ctxT[0:rows_k, k, a * bpt:(a + 1) * bpt, half, :],
                            banks[bank][0:rows_k, 0:PART].rearrange("p (b m) -> p b m", b=bpt)),
                            (t,), "ctx_copied")
                    freed[bank] = t2
            order = ["S0a", "S0b", "S1a", "S1b"]
            n = 0
            for p in range(PAIRS):
                bank = order[n % 4]
                n += 1

                def keys(e, p=p, bank=bank):
                    for k, rows_k in ((0, PART), (1, CREST)):
                        last = e.matmul(banks[bank][:, 0:B * M], wk2[0:rows_k, k, p * PART:(p + 1) * PART],
                                        ctxT[0:rows_k, k, :, 0, :], start=(k == 0), stop=(k == 1))
                    return last
                t = put("tensor", keys, (t2, wkv2_in, *both(bank)), "ctx_product")
                done = []
                for half, engine in ((0, "vector"), (1, "scalar")):
                    r0, r1 = half * DH, (half + 1) * DH
                    src = banks[bank][r0:r1, 0:B * M].rearrange("p (b m) -> p b m", b=B)
                    dst = stage[r0:r1, :, 0, p, r0:r1]
                    f = (lambda e, dst=dst, src=src: e.tensor_copy(dst, src)) if engine == "vector" else \
                        (lambda e, dst=dst, src=src: e.copy(dst, src))
                    done.append(put(engine, f, (t, stage_zero), f"ctx_{engine}"))
                freed[bank] = done[0]
                freed[bank + "+"] = done[1]
            return done, n, order

        def both(bank):
            return (freed[bank], freed.pop(bank + "+", None))

        def context_values(keys_done, n, order):
            done = keys_done
            for b in range(B):
                for h in range(INNER // BANK):
                    bank = order[n % 4]
                    n += 1

                    def values(e, b=b, h=h, bank=bank):
                        for k, rows_k in ((0, PART), (1, CREST)):
                            last = e.matmul(banks[bank], ctxT[0:rows_k, k, b, :, :],
                                            wv2[0:rows_k, k, h * BANK:(h + 1) * BANK],
                                            start=(k == 0), stop=(k == 1))
                        return last
                    t = put("tensor", values, (wkv2_in, *both(bank)), "ctx_product")
                    done = []
                    pp = BANK // PART
                    for half, engine in ((0, "vector"), (1, "scalar")):
                        r0, r1 = half * DH, (half + 1) * DH
                        src = banks[bank][r0:r1, :].rearrange("p (q n) -> p q n", q=pp)[:, :, r0:r1]
                        dst = stage[r0:r1, b, 1, h * pp:(h + 1) * pp, r0:r1]
                        f = (lambda e, dst=dst, src=src: e.tensor_copy(dst, src)) if engine == "vector" else \
                            (lambda e, dst=dst, src=src: e.copy(dst, src))
                        done.append(put(engine, f, (t, stage_zero), f"ctx_{engine}"))
                    freed[bank] = done[0]
                    freed[bank + "+"] = done[1]
            t = dma(lambda e: e.dma_start(cross_dram.rearrange("b p n -> p b n"),
                                          ptflat.rearrange("p (b n) -> p b n", b=B)), done, "cross_stored")
            return t, done

        qkv_done = {}
        q_ready, k_ready, v_ready, k_dup = {}, {}, {}, {}
        s_done, t_done, pv_done = {}, {}, {}

        def project_qk(P, kind, c, h_ready):
            par = P % 2

            def product(e):
                for k in range(KT):
                    last = e.matmul(PJ[:, :], wqkv[:, par, kind, k, :], hT[:, k, c * BANK:(c + 1) * BANK],
                                    start=(k == 0), stop=(k == KT - 1))
                return last
            t = put("tensor", product, (wqkv_in[P], *h_ready, freed["PJ"]), "projected")
            span = slice(c * BANK, (c + 1) * BANK)
            tickets = []
            for head in range(2):
                r = slice(head * DH, (head + 1) * DH)
                o = slice((1 - head) * DH, (2 - head) * DH)
                hi = qk[r, par, head, 0 if kind == 0 else 1, span]
                lo = qk[o, par, head, 0, span] if kind == 0 else qk[r, par, head, 2, span]
                scale = SCALE if kind == 0 else 1.0
                a = put("scalar", lambda e, hi=hi, r=r, scale=scale: e.activation(
                    hi, PJ[r, :], ACT.Copy, scale=scale), (t, s_done.get(f"pair{P - 2}"), k_dup.get(P - 2)), "split_hi")
                tickets.append((head, r, hi, lo, scale, a))
            for head, r, hi, lo, scale, a in tickets:
                d = put("vector", lambda e, r=r, hi=hi, lo=lo, scale=scale: e.scalar_tensor_tensor(
                    lo, PJ[r, :], scale, hi.bitcast(F32), ALU.mult, ALU.subtract), (a,), "split_lo")
            freed["PJ"] = d
            (q_ready if kind == 0 else k_ready)[P] = (a, d)
            qkv_done[P] = t

        def duplicate_k(P):
            for head in range(2):
                r, o = slice(head * DH, (head + 1) * DH), slice((1 - head) * DH, (2 - head) * DH)
                t = dma(lambda e, head=head, r=r, o=o: e.dma_start(
                    qk[o, P % 2, head, 1:3, :].bitcast(F32), qk[r, P % 2, head, 1:3, :].bitcast(F32)), k_ready[P], f"k_doubled{P % 2}")
            k_dup[P] = t

        def project_v(P, c, h_ready):
            def product(e):
                for j in range(TPC):
                    t = c * TPC + j
                    for k in range(KT):
                        last = e.matmul(PJ[:, j * PART:(j + 1) * PART], hT[:, k, t * PART:(t + 1) * PART],
                                        wqkv[:, P % 2, 2, k, :], start=(k == 0), stop=(k == KT - 1))
                return last
            t = put("tensor", product, (wqkv_in[P], *h_ready, freed["PJ"]), "projected")
            dst = v_sb[:, P % 2, c * TPC:(c + 1) * TPC, :].rearrange("p t n -> p (t n)")
            freed["PJ"] = v_ready[P] = put("vector", lambda e: e.tensor_copy(dst, PJ[:, :]),
                                           (t, pv_done.get(P - 2)), "v_copied")
            qkv_done[P] = t

        def projections(P, u, h_ready):
            if u < 4:
                project_qk(P, 1 if u < 2 else 0, u % 2, h_ready)
                if u == 1:
                    duplicate_k(P)
            else:
                project_v(P, u - 4, h_ready)

        norm_done, exp_done, max_done, turn_read, pT_written, o_written = {}, {}, {}, {}, {}, {}

        def score(n):
            P, it, head = n // (2 * TILES), n // 2 % TILES, n % 2
            a = f"S{n % 2}a", f"S{n % 2}b"

            def product(e):
                q = qk[:, P % 2, head, 0, it * PART:(it + 1) * PART]
                for half in range(2):
                    for part in (1, 2):
                        last = e.matmul(SC[n % 2][:, half * BANK:(half + 1) * BANK], q,
                                        qk[:, P % 2, head, part, half * BANK:(half + 1) * BANK],
                                        start=(part == 1), stop=(part == 2))
                return last
            waits = (*q_ready[P], *k_ready[P], k_dup[P], freed[a[0]], freed[a[1]],
                     freed.pop(a[0] + "+", None), freed.pop(a[1] + "+", None))
            s_done[n] = put("tensor", product, waits, "scored")
            if it == TILES - 1 and head == 1:
                s_done[f"pair{P}"] = s_done[n]

        def row_max(n):
            max_done[n] = put("vector", lambda e: e.tensor_reduce(
                nmax[:, n % 8:n % 8 + 1], SC[n % 2][:, :], AX.X, ALU.max, negate=True), (s_done[n],), "row_max")

        def exponential(n):
            exp_done[n] = put("scalar", lambda e: e.activation(
                probs[:, n % 3, :], SC[n % 2][:, :], ACT.Exp, bias=nmax[:, n % 8:n % 8 + 1],
                accum_out=lsum[:, n % 8:n % 8 + 1]), (max_done[n], t_done.get(n - 3)), "exponential")
            freed[f"S{n % 2}a"] = freed[f"S{n % 2}b"] = exp_done[n]

        def normalise(n):
            t = put("vector", lambda e: e.reciprocal(rsum[:, n % 8:n % 8 + 1], lsum[:, n % 8:n % 8 + 1]),
                    (exp_done[n],), "row_sum")
            norm_done[n] = put("gpsimd", lambda e: e.tensor_scalar(
                probs[:, n % 3, :], probs[:, n % 3, :], rsum[:, n % 8:n % 8 + 1], 1.0, ALU.mult, ALU.mult),
                (t, exp_done[n]), "normalised")

        def turn(n):
            g, it, head = n // 4, n // 2 % 2, n % 2
            for half in range(2):
                bank = f"T{half}"

                def product(e, half=half, bank=bank):
                    for j in range(4):
                        jt = half * 4 + j
                        last = e.transpose(banks[bank][:, j * PART:(j + 1) * PART],
                                           probs[:, n % 3, jt * PART:(jt + 1) * PART], ident[:, :])
                    return last
                t_done[n] = put("tensor", product, (norm_done[n], freed[bank]), "turned")
                dst = pT[:, g % 2, head, half * 4:half * 4 + 4, it * PART:(it + 1) * PART]
                src = banks[bank].rearrange("p (j n) -> p j n", j=4)
                waits = (t_done[n], pv_done.get(("group", g - 2)), cross_stored[0])
                if half == 0:
                    t = put("scalar", lambda e, dst=dst, src=src: e.copy(dst, src), waits, "pT_act")
                else:
                    t = put("vector", lambda e, dst=dst, src=src: e.tensor_copy(dst, src), waits, "pT_dve")
                freed[bank] = t
                pT_written[n, half] = t

        def attend(g, part):
            P = g * 4 // (2 * TILES)
            jts = range(part * TILES // 4, (part + 1) * TILES // 4)

            def product(e):
                for jt in jts:
                    for head in range(2):
                        r = slice(head * DH, (head + 1) * DH)
                        last = e.matmul(PV[r, 0:2 * PART], v_sb[:, P % 2, jt, r],
                                        pT[:, g % 2, head, jt, :], start=(jt == 0), stop=(jt == TILES - 1))
                return last
            waits = [v_ready[P], freed["PV"]] + [pT_written[4 * g + i, h] for i in range(4) for h in range(2)]
            t = put("tensor", product, waits, "attended")
            if part == 3:
                pv_done["group", g] = pv_done[P] = t
                i0 = (g * 2 % TILES) * PART
                freed["PV"] = o_written[P] = put("scalar", lambda e: e.copy(
                    oT[:, P % PAIRS, i0:i0 + 2 * PART], PV[:, 0:2 * PART]), (t, oT_free[0]), "oT_written")

        cross_stored = [None]
        oT_free = [None]
        steps = PAIRS * 2 * TILES

        def self_attention(b, h_ready):
            P0, n0 = b * PAIRS, b * steps
            for u in range(6):
                projections(P0, u, h_ready)
            slot_of_unit = {2 + 2 * u: u for u in range(6)}
            for i in range(steps + 10):
                n, p = n0 + i, i // (2 * TILES)
                if i < steps:
                    score(n)
                if 0 <= i - 1 < steps:
                    normalise(n - 1)
                if i < steps:
                    row_max(n)
                if 0 <= i - 2 < steps:
                    turn(n - 2)
                if i < steps:
                    exponential(n)
                j = i - 6
                if 0 <= j < steps:
                    attend((n0 + j) // 4, j % 4)
                if i < steps and p + 1 < PAIRS and i % (2 * TILES) in slot_of_unit:
                    projections(P0 + p + 1, slot_of_unit[i % (2 * TILES)], h_ready)
                if i < steps and i % (2 * TILES) == 2 * TILES - 1 and P0 + p + 2 < B * PAIRS:
                    P = P0 + p + 2
                    wqkv_in[P] = load_wqkv(P, (qkv_done[P - 2],))

        def output(b, t, src, w, bank, extra, name):
            def product(e):
                for p in range(PAIRS):
                    last = e.matmul(banks[bank][:, 0:DIM], src(p), w[:, p, :], start=(p == 0),
                                    stop=(p == PAIRS - 1))
                return last
            m = put("tensor", product, (*extra, freed[bank]), "out_product")
            freed[bank] = put("vector", lambda e: e.tensor_tensor(
                xres[:, b % 2, t, :], banks[bank][:, 0:DIM], xres[:, b % 2, t, :], ALU.add),
                (m, bias_added[0]), name)
            return m, freed[bank]

        bias_added = [None]

        def add_bias(b, i, waits):
            for t in range(TILES):
                bias_added[0] = put("gpsimd", lambda e, t=t: e.tensor_tensor(
                    xres[:, b % 2, t, :], xres[:, b % 2, t, :], rows[:, i, :], ALU.add),
                    (*waits, rows_in), "bias_added")

        def cross_attention(b, h_ready, cross_in):
            ring = ["S0a", "S0b", "S1a", "S1b", "PV", "PJ"]
            q2_ready = {}
            n = 0
            for c in range(CHUNKS):
                for p in range(PAIRS):
                    bank = ring[n % 6]
                    n += 1

                    def product(e, c=c, p=p, bank=bank):
                        for k in range(KT):
                            last = e.matmul(banks[bank], wq2[:, k, p * PART:(p + 1) * PART],
                                            hT[:, k, c * BANK:(c + 1) * BANK], start=(k == 0), stop=(k == KT - 1))
                        return last
                    m = put("tensor", product, (*h_ready[c], w_in, freed[bank]), "q2_product")
                    dst = q2T[:, p, c * BANK:(c + 1) * BANK]
                    if n % 2:
                        t = put("scalar", lambda e, dst=dst, bank=bank: e.activation(
                            dst, banks[bank], ACT.Copy, scale=SCALE), (m, oT_free[0]), "q2_act")
                    else:
                        t = put("vector", lambda e, dst=dst, bank=bank: e.tensor_scalar(
                            dst, banks[bank], SCALE, None, ALU.mult), (m, oT_free[0]), "q2_dve")
                    freed[bank] = t
                    q2_ready[c, n % 2] = t
            p2_scaled, p2T_ready, o2T_ready = {}, {}, {}
            x_done = {}

            def score2(t):
                c = t // TPC

                def product(e):
                    for p in range(PAIRS):
                        last = e.matmul(SC[t % 2][:, p * PART:(p + 1) * PART], q2T[:, p, t * PART:(t + 1) * PART],
                                        cross[:, 0, p, :], start=True, stop=True)
                    return last
                s = put("tensor", product, (q2_ready[c, 0], q2_ready[c, 1], cross_in, freed[f"S{t % 2}a"],
                                            freed[f"S{t % 2}b"]), "scored2")
                s3 = SC[t % 2][:, :].rearrange("p (h m) -> p h m", h=HEADS)
                P3 = probs[:, t % 3, :].rearrange("p (h m) -> p h m", h=HEADS)
                nm = nmax2[:, t % 2, :]
                mx = put("vector", lambda e: e.tensor_reduce(nm, s3, AX.X, ALU.max, negate=True), (s,), "soft2")
                sub = put("vector", lambda e: e.tensor_tensor(
                    P3, s3, nm.unsqueeze(2).to_broadcast([PART, HEADS, M]), ALU.add),
                    (mx, p2_read.get(t - 3)), "soft2")
                freed[f"S{t % 2}a"] = freed[f"S{t % 2}b"] = sub
                ex = put("scalar", lambda e: e.activation(probs[:, t % 3, :], probs[:, t % 3, :], ACT.Exp),
                         (sub,), "exp2")
                exp2[t] = ex

            def soften2(t):
                P3 = probs[:, t % 3, :].rearrange("p (h m) -> p h m", h=HEADS)
                ls, rr = lsum2[:, t % 2, :], rsum2[:, t % 2, :]
                su = put("vector", lambda e: e.tensor_reduce(ls, P3, AX.X, ALU.add), (exp2[t],), "soft2")
                rc = put("vector", lambda e: e.reciprocal(rr, ls), (su,), "soft2")
                p2_scaled[t] = put("vector", lambda e: e.tensor_tensor(
                    P3, P3, rr.unsqueeze(2).to_broadcast([PART, HEADS, M]), ALU.mult), (rc,), "soft2")

            def turn2(t):
                c = t // TPC
                for half in range(2):
                    bank = f"T{half}"

                    def product(e, half=half, bank=bank):
                        for j in range(4):
                            p = half * 4 + j
                            last = e.transpose(banks[bank][:, j * PART:(j + 1) * PART],
                                               probs[:, t % 3, p * PART:(p + 1) * PART], ident[:, :])
                        return last
                    m = put("tensor", product, (p2_scaled[t], freed[bank]), "turned2")
                    p2_read[t] = m
                    dst = p2T[:, c, half * 4:half * 4 + 4, (t % TPC) * PART:(t % TPC + 1) * PART]
                    src = banks[bank].rearrange("p (j n) -> p j n", j=4)
                    w = put("scalar", lambda e, dst=dst, src=src: e.copy(dst, src), (m,), "p2T_act")
                    freed[bank] = w
                    p2T_ready[c] = w

            def attend2(c, p):
                bank = ("PV", "PJ")[p % 2]
                m = put("tensor", lambda e: e.matmul(banks[bank], cross[:, 1, p, :], p2T[:, c, p, :],
                                                     start=True, stop=True),
                        (p2T_ready[c], freed[bank], cross_in), "attended2")
                cross_read[0] = m
                t = put("scalar", lambda e: e.copy(o2T[:, p, :], banks[bank]), (m, wo2_read.get(c - 1)), "o2T_act")
                freed[bank] = t
                o2T_ready[c] = t

            def out2(t):
                c = t // TPC
                m, added = output(b, t, lambda p: o2T[:, p, (t % TPC) * PART:(t % TPC + 1) * PART], wo2,
                                  ("PV", "PJ")[t % 2], (o2T_ready[c], w_in), "x2_added")
                wo2_read[c] = m
                x_done[t] = added

            p2_read, exp2, wo2_read = {}, {}, {}
            for i in range(TILES + 2):
                if i < TILES:
                    score2(i)
                if 0 <= i - 1 < TILES:
                    soften2(i - 1)
                if 0 <= i - 2 < TILES:
                    turn2(i - 2)
                if i - 2 == TPC - 1:
                    for p in range(PAIRS):
                        attend2(0, p)
                    for t in range(TPC):
                        out2(t)
            for p in range(PAIRS):
                attend2(1, p)
            for t in range(TPC, TILES):
                out2(t)
            return x_done

        cross_read = [None]

        hT_ready, _ = layer_norm(0, 0, [x_in[0]] * TILES, 0, None)
        keys_done, nbank, order = context()
        cross_stored[0], stage_done = context_values(keys_done, nbank, order)
        x_stored, x_read = {}, {}
        for b in range(B):
            if b:
                hT_ready, _ = layer_norm(b, 0, [x_in[b]] * TILES, 0, hT_read[0])
            h_all = [t for c in range(CHUNKS) for t in hT_ready[c]]
            cross_in = dma(lambda e, b=b: e.dma_start(
                cross[:, :, :, :].rearrange("p w q n -> p (w q n)"), cross_dram[b]),
                (cross_stored[0], cross_read[0]), "cross_loaded")
            if b + 1 < B:
                x_in[b + 1] = load_x(b + 1, (x_stored.get(b - 1), x_read.get(b - 1)))
            add_bias(b, 0, h_all)
            self_attention(b, h_all)
            ring = ["S0a", "S0b", "S1a", "S1b", "PV", "PJ"]
            x_new = {}
            for t in range(TILES):
                m, x_new[t] = output(b, t, lambda p, t=t: oT[:, p, t * PART:(t + 1) * PART], wo1, ring[t % 6],
                                     (o_written[b * PAIRS + PAIRS - 1], w_in), "x1_added")
            oT_free[0] = m
            hT2_ready, _ = layer_norm(b, 1, [x_new[t] for t in range(TILES)], 0, qkv_done[b * PAIRS + PAIRS - 1])
            add_bias(b, 1, [t for c in range(CHUNKS) for t in hT2_ready[c]])
            x_done = cross_attention(b, hT2_ready, cross_in)
            hT_read = [("q2_product", Q.raised["q2_product"])]
            oT_free[0] = ("scored2", Q.raised["scored2"])
            agg = ln_stats(lambda t, b=b: xres[:, b % 2, t, :], TILES, lambda t, b=b: mv3[:, b, t, :], 0,
                           [x_done[t] for t in range(TILES)])
            x_read[b] = agg
            x_stored[b] = dma(lambda e, b=b: e.dma_start(xmid[b], xres[:, b % 2]), (x_done[TILES - 1],),
                              f"x_stored{b % 2}")

        last_pv = pv_done["group", B * steps // 4 - 1]
        dma(lambda e: e.dma_start(wp, Wp.rearrange("(k p) n -> p k n", p=PART)), (last_pv,), "ffn_loaded")
        ffn_in = dma(lambda e: e.dma_start(w2, W2.rearrange("(f p) n -> p f n", p=PART)), (last_pv,), "ffn_loaded")
        r3 = ln_rstd(mv3[:, :, :, 1].rearrange("p b t -> p (b t)"), 0, B * TILES, (agg,))
        NCH = B * CHUNKS
        oT_last = (("scored2", Q.raised["scored2"]),)
        qk_last = (("out_product", Q.raised["out_product"]),)
        xf_in, biased, h3, u_ready, w2_read, xf_read, gate_read, stored = {}, {}, {}, {}, {}, {}, {}, {}
        a_read = {}

        def load_chunk(c):
            b, t0 = c // CHUNKS, (c % CHUNKS) * TPC
            xf_in[c] = dma(lambda e: e.dma_start(xf[:, c % 3], xmid[b, :, t0:t0 + TPC, :]),
                           (*oT_last, x_stored[b], x_stored[B - 1], xf_read.get(c - 3), xf_in.get(c - 3)), f"xf_loaded{c % 3}")

        def chunk_rows(c):
            b, t0 = c // CHUNKS, (c % CHUNKS) * TPC
            slots = []
            for j in range(TPC):
                s, t = ln_rows(xf[:, c % 3, j, :], mv3[:, b, t0 + j, 0:1],
                               rs[:, b * TILES + t0 + j:b * TILES + t0 + j + 1], (r3, xf_in[c]))
                slots.append((s, t))
            h3[c] = ln_turn(c % 2, slots, 2, a_read.get(c - 2, hT_read[0]))
            for j in range(TPC):
                biased[c] = put("gpsimd", lambda e, j=j: e.tensor_tensor(
                    xf[:, c % 3, j, :], xf[:, c % 3, j, :], rows[:, 2, :], ALU.add), (slots[-1][1],), "bias3_added")

        def ffn_up(c, f):
            for which, bank in ((1, ("S0a", "S1a")[f % 2]), (0, ("S0b", "S1b")[f % 2])):
                col = which * FT + f

                def product(e, col=col, bank=bank):
                    for k in range(KT):
                        last = e.matmul(banks[bank], wp[:, k, col * PART:(col + 1) * PART],
                                        hT[:, k, (c % 2) * BANK:(c % 2 + 1) * BANK], start=(k == 0),
                                        stop=(k == KT - 1))
                    return last
                m = put("tensor", product, (*h3[c], ffn_in, freed[bank]), "up_product")
                i = c * FT + f
                if which == 1:
                    g = put("scalar", lambda e, bank=bank, col=col, i=i: e.activation(
                        gate[:, i % 3, :], banks[bank], ACT.Gelu, bias=bp_col[:, col:col + 1]),
                        (m, bp_in, gate_read.get(i - 3), *oT_last), "gelu")
                    freed[bank] = g
                else:
                    u = put("vector", lambda e, bank=bank, col=col, i=i: e.scalar_tensor_tensor(
                        uT[:, c % 2, f, :], banks[bank], bp_col[:, col:col + 1], gate[:, i % 3, :],
                        ALU.add, ALU.mult), (m, g, w2_read.get(c - 2), *qk_last), "gated")
                    freed[bank] = gate_read[i] = u_ready[c] = u
            a_read[c] = m

        def ffn_down(c, j):
            b, t0 = c // CHUNKS, (c % CHUNKS) * TPC
            bank = ("PV", "PJ")[j % 2]

            def product(e):
                for f in range(FT):
                    last = e.matmul(banks[bank][:, 0:DIM], uT[:, c % 2, f, j * PART:(j + 1) * PART], w2[:, f, :],
                                    start=(f == 0), stop=(f == FT - 1))
                return last
            m = put("tensor", product, (u_ready[c], freed[bank]), "down_product")
            w2_read[c] = m
            y = put("vector", lambda e: e.tensor_tensor(yf[:, c % 2, j, :], banks[bank][:, 0:DIM],
                                                        xf[:, c % 3, j, :], ALU.add),
                    (m, biased[c], stored.get(c - 2)), "y_added")
            freed[bank] = y
            if j == TPC - 1:
                xf_read[c] = y
                dst = out[b, t0 * PART:(t0 + TPC) * PART, :].rearrange("(t p) d -> p t d", p=PART)
                stored[c] = dma(lambda e: e.dma_start(dst, yf[:, c % 2]), (y,), f"y_stored{c % 2}")

        for c in range(2):
            load_chunk(c)
        chunk_rows(0)
        for c in range(NCH + 1):
            for f in range(FT):
                if c < NCH:
                    ffn_up(c, f)
                if f == 3 and c + 1 < NCH:
                    chunk_rows(c + 1)
                if c and f % 2 == 1:
                    ffn_down(c - 1, f // 2)
            if c + 2 < NCH:
                load_chunk(c + 2)

        block = stack.enter_context(nc.Block())

        @block.tensor
        def _(e):
            Q.play("tensor", e)

        @block.vector
        def _(e):
            Q.play("vector", e)

        @block.scalar
        def _(e):
            Q.play("scalar", e)

        @block.gpsimd
        def _(e):
            Q.play("gpsimd", e)

        @block.sync
        def _(e):
            Q.play("sync", e)
            for name in ("cross_stored", "x_stored0", "x_stored1", "y_stored0", "y_stored1"):
                e.wait_ge(semaphore(name), Q.raised[name])


_NAMES = ["x", "ctx_768"] + ["L0_xattn_" + n for n in (
    "Wq1 Wk1 Wv1 Wo1 bo1 Wq2 Wk2 Wv2 Wo2 bo2 Wp bp W2 b2 g1 be1 g2 be2 g3 be3").split()]


def kernel(**inputs):
    import numpy as np
    import concourse.bacc as bacc
    from concourse import mybir as mb
    from concourse.bass_utils import run_bass_kernel_spmd

    nc = bacc.Bacc("TRN2", target_bir_lowering=False, num_devices=1)
    arrays, args = {}, []
    for name in _NAMES:
        a = np.ascontiguousarray(inputs[name])
        arrays[f"in_{name}"] = a
        args.append(nc.dram_tensor(f"in_{name}", a.shape, mb.dt.from_np(a.dtype), kind="ExternalInput").ap())
    shape = inputs["x"].shape
    args.append(nc.dram_tensor("out_x", shape, mb.dt.float32, kind="ExternalOutput").ap())
    block_kernel(nc, *args)
    r = run_bass_kernel_spmd(nc, [arrays], core_ids=[0])
    return r.results[0]["out_x"]
```

```python
from contextlib import ExitStack

import concourse.bass as bass
from concourse import mybir
from concourse.alu_op_type import AluOpType as ALU

F32 = mybir.dt.float32
F32R = mybir.dt.float32r
ACT = mybir.ActivationFunctionType
AX = mybir.AxisListType

PART = 128
BANK = 512
EPS = 1e-5


class Queues:

    def __init__(self, semaphore):
        self.semaphore = semaphore
        self.streams = {"tensor": [], "vector": [], "scalar": [], "gpsimd": [], "sync": []}
        self.raised = {}

    def put(self, engine, emit, waits=(), signal=None, step=1):
        ticket = None
        if signal is not None:
            self.raised[signal] = self.raised.get(signal, 0) + step
            ticket = (signal, self.raised[signal])
        self.streams[engine].append((emit, waits, signal, step))
        return ticket

    def dma(self, emit, waits=(), signal=None):
        return self.put("sync", emit, waits, signal, 16)

    def play(self, name, engine):
        seen = {}
        for emit, waits, signal, step in self.streams[name]:
            for ticket in waits:
                if ticket is not None and seen.get(ticket[0], 0) < ticket[1]:
                    engine.wait_ge(self.semaphore(ticket[0]), ticket[1])
                    seen[ticket[0]] = ticket[1]
            last = emit(engine)
            if signal is not None:
                last.then_inc(self.semaphore(signal), step)


def block_kernel(nc, x, ctx, Wq1, Wk1, Wv1, Wo1, bo1, Wq2, Wk2, Wv2, Wo2, bo2, Wp, bp, W2, b2,
                 g1, be1, g2, be2, g3, be3, out):
    B, N, DIM = x.shape
    M, CD = ctx.shape[1:]
    INNER = Wq1.shape[1]
    DH = 64
    HEADS = INNER // DH
    SCALE = DH ** -0.5
    FF = W2.shape[0]
    KT = DIM // PART
    PAIRS = HEADS // 2
    TILES = N // PART
    CHUNKS = N // BANK
    TPC = BANK // PART
    FT = FF // PART
    CREST = CD - PART

    stack = ExitStack()
    with stack:
        def sb(name, shape, dt=F32):
            return stack.enter_context(nc.sbuf_tensor(name, shape, dt))

        def ps(name, shape):
            return stack.enter_context(nc.psum_tensor(name, shape, F32))

        ident = sb("ident", [PART, PART])
        eps = sb("eps", [PART, 1])
        cols = sb("cols", [PART, 6, KT])
        bp_col = sb("bp_col", [PART, 2 * FT])
        rows = sb("rows", [PART, 3, DIM])
        xres = sb("xres", [PART, 2, TILES, DIM])
        hT = sb("hT", [PART, 2, KT, N], F32R)
        xn = sb("xn", [PART, TPC, DIM])
        stats = sb("stats", [PART, TILES, 6])
        mv1 = sb("mv1", [PART, TILES, 2])
        mv2 = sb("mv2", [PART, TILES, 2])
        mv3 = sb("mv3", [PART, B, TILES, 2])
        sd = sb("sd", [PART, B * TILES])
        rs1 = sb("rs1", [PART, TILES])
        rs2 = sb("rs2", [PART, TILES])
        rs3 = sb("rs3", [PART, B * TILES])
        nmax = sb("nmax", [PART, 8])
        lsum = sb("lsum", [PART, 8])
        rsum = sb("rsum", [PART, 8])
        nmax2 = sb("nmax2", [PART, 2, HEADS])
        lsum2 = sb("lsum2", [PART, 2, HEADS])
        rsum2 = sb("rsum2", [PART, 2, HEADS])

        def overlay(*specs):
            with ExitStack() as scope:
                return [scope.enter_context(nc.sbuf_tensor(n, [PART, *shape], dt)) for n, shape, dt in specs]

        (oT, pT, qk, probs, v_sb, raw_qk, wqk, raw_v, wv, wo1) = overlay(
            ("oT", [PAIRS, N], F32),
            ("pT", [2, 2, TILES, 2 * PART], F32),
            ("qk", [2, 2, 3, N], F32R),
            ("probs", [3, N], F32),
            ("v_sb", [TILES, 2 * PART], F32),
            ("raw_qk", [2, KT, PART], F32),
            ("wqk", [2, 2, 2, KT, PART], F32R),
            ("raw_v", [KT, 2 * PART], F32),
            ("wv", [2, KT, 2 * PART], F32R),
            ("wo1", [2, PAIRS, DIM], F32R))
        (wkv2, wq2, wq2T, ctx_sb, ctxT, wo2, diag, keys2) = overlay(
            ("wkv2", [2, 2, INNER], F32),
            ("wq2", [KT, INNER], F32),
            ("wq2T", [PAIRS, DIM], F32),
            ("ctx_sb", [2, CD], F32),
            ("ctxT", [2, B, M], F32),
            ("wo2", [PAIRS, DIM], F32),
            ("diag", [2, B, PAIRS, PART], F32),
            ("keys2", [B, KT, INNER], F32))
        (values2,) = overlay(("values2", [B, PAIRS, DIM], F32))
        (_, cross, turned, raw_cross) = overlay(
            ("oT_kept", [PAIRS, N], F32),
            ("cross", [2, 2, 2 * INNER], F32R),
            ("turned", [3, 2, PAIRS, PART], F32R),
            ("raw_cross", [2, 2 * INNER], F32))
        keys_hl = cross[:, 0].rearrange("p w (k n) -> p w k n", k=KT)
        values_hl = cross[:, 1].rearrange("p w (q n) -> p w q n", q=PAIRS)
        (raw_wp, raw_w2, gate, wp, w2, uT) = overlay(
            ("raw_wp", [KT, 2 * FF], F32), ("raw_w2", [FT, DIM], F32), ("gate", [4, BANK], F32),
            ("wp", [2, KT, 2 * FF], F32R), ("w2", [2, FT, DIM], F32R), ("uT", [2, 2, FT, BANK], F32R))
        (_, u_full) = overlay(("ffn_kept", [KT * 2 * FF + FT * DIM + 4 * BANK + 2 * KT * 2 * FF
                                        + 2 * FT * DIM + 4 * FT * BANK], F32), ("u_full", [3, BANK], F32))
        xf = xres[:, :, :, :].rearrange("p a (c t) n -> p (a c) t n", t=TPC)

        SC = [ps(f"score{i}", [PART, 2 * BANK]) for i in range(2)]
        TP = [ps(f"turn{i}", [PART, BANK]) for i in range(2)]
        PV = ps("attn_out", [PART, BANK])
        PJ = ps("project", [PART, BANK])
        banks = {"S0a": SC[0][:, 0:BANK], "S0b": SC[0][:, BANK:], "S1a": SC[1][:, 0:BANK],
                 "S1b": SC[1][:, BANK:], "T0": TP[0][:, :], "T1": TP[1][:, :], "PV": PV[:, :], "PJ": PJ[:, :]}
        freed = {name: () for name in banks}

        cross_dram = nc.dram_tensor("cross_tiles", (B, PART, 2, 2 * INNER), F32, kind="Internal").ap()
        xmid = nc.dram_tensor("x_middle", (B, PART, TILES, DIM), F32, kind="Internal").ap()

        sems = {}

        def semaphore(name):
            if name not in sems:
                sems[name] = stack.enter_context(nc.semaphore(name))
            return sems[name]

        Q = Queues(semaphore)
        put, dma = Q.put, Q.dma

        def load_x(b, waits=()):
            return dma(lambda e: e.dma_start(xres[:, b % 2], x[b].rearrange("(t p) d -> p t d", p=PART)),
                       waits, f"x_loaded{b % 2}")

        raw_qk_read, raw_v_read = [None], [None]
        qk_done, v_done = {}, {}
        wqk_in, wv_in = {}, {}

        def split_weights(raw, hi, lo, loaded, buffer_free, name):
            h = put("gpsimd", lambda e: e.tensor_scalar(hi, raw, 1.0, 1.0, ALU.mult, ALU.mult),
                    (loaded, buffer_free), name)
            return put("gpsimd", lambda e: e.tensor_tensor(lo, raw, hi.bitcast(F32), ALU.subtract), (h,), name)

        def stream_qk(P):
            c = (P % PAIRS) * PART
            for i, w in enumerate((Wq1, Wk1)):
                src = w.rearrange("(k p) n -> p k n", p=PART)[:, :, c:c + PART]
                t = dma(lambda e, i=i, src=src: e.dma_start(raw_qk[:, i], src), (raw_qk_read[0],), "wqk_loaded")
            flat = "p i k n -> p (i k n)"
            raw_qk_read[0] = wqk_in[P] = split_weights(
                raw_qk[:, :, :, :].rearrange(flat), wqk[:, P % 2, 0].rearrange(flat),
                wqk[:, P % 2, 1].rearrange(flat), t, qk_done.get(P - 2), "wqk_split")

        def stream_v(D):
            c = (D % (PAIRS // 2)) * 2 * PART
            src = Wv1.rearrange("(k p) n -> p k n", p=PART)[:, :, c:c + 2 * PART]
            t = dma(lambda e: e.dma_start(raw_v[:, :, :], src), (raw_v_read[0],), "wv_loaded")
            flat = "p k n -> p (k n)"
            raw_v_read[0] = wv_in[D] = split_weights(
                raw_v[:, :, :].rearrange(flat), wv[:, 0].rearrange(flat), wv[:, 1].rearrange(flat), t,
                v_done.get(D - 1), "wv_split")

        x_in = {0: load_x(0)}
        for i, v in enumerate((g1, be1, g2, be2, g3, be3)):
            cols_in = dma(lambda e, i=i, v=v: e.dma_start(cols[:, i, :], v.rearrange("(k p) -> p k", p=PART),
                                                          allow_slow_non_contiguous=True), signal="cols_loaded")
        ctx_rows = ctx.rearrange("b m c -> (b m) c").rearrange("(a p) c -> p a c", p=PART)
        ctx_in = dma(lambda e: e.dma_start(ctx_sb[:, :, :], ctx_rows), signal="ctx_loaded")
        t = put("gpsimd", lambda e: e.memset(ident[:, :], 0.0), signal="const")
        ident_in = put("gpsimd", lambda e: e.affine_select(
            out=ident[:, :], in_=ident[:, :], compare_op=ALU.not_equal, fill=1.0, base=0,
            pattern=[[-1, PART]], channel_multiplier=1), (t,), "const")
        eps_in = put("gpsimd", lambda e: e.memset(eps[:, :], EPS), signal="const")
        diag_flat = diag[:, :, :, :, :].rearrange("p w b q n -> p (w b q n)")
        half = 2 * B * PAIRS * PART // 2
        zero_a = put("gpsimd", lambda e: e.memset(diag_flat[:, 0:half], 0.0), signal="const")
        zero_b = put("vector", lambda e: e.memset(diag_flat[:, half:2 * half], 0.0), signal="const_dve")
        stream_qk(0)
        stream_v(0)
        for i, w in enumerate((Wk2, Wv2)):
            dma(lambda e, i=i, w=w: e.dma_start(wkv2[:, i, 0], w[0:PART]), signal="wkv2_loaded")
            wkv2_in = dma(lambda e, i=i, w=w: e.dma_start(wkv2[0:CREST, i, 1], w[PART:CD]), signal="wkv2_loaded")
        wq2_in = dma(lambda e: e.dma_start(wq2[:, :, :], Wq2.rearrange("(k p) n -> p k n", p=PART)),
                     signal="wq2_loaded")
        wo2_in = dma(lambda e: e.dma_start(wo2[:, :, :], Wo2.rearrange("(q p) n -> p q n", p=PART)),
                     signal="wo2_loaded")
        stream_qk(1)
        raw_wo1 = xres[:, 1].rearrange("p t n -> p (t n)")
        wo1_raw_in = dma(lambda e: e.dma_start(raw_wo1.rearrange("p (q n) -> p q n", q=PAIRS),
                                               Wo1.rearrange("(q p) n -> p q n", p=PART)), signal="wo1_loaded")
        for i, v in enumerate((bo1, bo2, b2)):
            rows_in = dma(lambda e, i=i, v=v: e.dma_start(
                rows[:, i, :], v.rearrange("(a n) -> a n", a=1).to_broadcast([PART, DIM])), signal="rows_loaded")
        bp_in = dma(lambda e: e.dma_start(bp_col[:, :], bp.rearrange("(f p) -> p f", p=PART),
                                          allow_slow_non_contiguous=True), signal="bp_loaded")
        wo1_in = split_weights(raw_wo1, wo1[:, 0].rearrange("p q n -> p (q n)"),
                               wo1[:, 1].rearrange("p q n -> p (q n)"), wo1_raw_in, None, "wo1_split")

        stats_read = {}

        def ln_stats(src, mv_of, slot, ready):
            st = put("vector", lambda e: e.bn_stats(stats[:, slot, :], src), (ready, stats_read.get(slot)), "ln_stat")
            stats_read[slot] = put("vector", lambda e: e.bn_aggr(mv_of, stats[:, slot, :]), (st,), "ln_stat")
            return stats_read[slot]

        sd_read = [None]

        def ln_rstd(var, rs, waits):
            n = var.shape[-1]
            root = put("scalar", lambda e: e.activation(sd[:, 0:n], var, ACT.Sqrt, bias=eps[:, 0:1]),
                       (*waits, eps_in, sd_read[0]), "ln_root")
            sd_read[0] = put("vector", lambda e: e.reciprocal(rs, sd[:, 0:n]), (root,), "ln_stat")
            return sd_read[0]

        xn_read = {}

        def ln_rows(tiles, waits):
            for slot, (src, mean, r) in enumerate(tiles):
                t = put("vector", lambda e, slot=slot, src=src, mean=mean, r=r: e.tensor_scalar(
                    xn[:, slot, :], src, mean, r, ALU.subtract, ALU.mult), (*waits, xn_read.get(slot)), "ln_rows")
            return t

        def ln_turn(c, ready, which, hT_free):
            done = []
            for k in range(KT):
                bank = f"T{k}"

                def product(e, k=k, bank=bank):
                    for j in range(TPC):
                        last = e.transpose(banks[bank][:, j * PART:(j + 1) * PART],
                                           xn[:, j, k * PART:(k + 1) * PART], ident[:, :])
                    return last
                m = put("tensor", product, (ready, ident_in, *freed[bank]), "ln_turned")
                for j in range(TPC):
                    xn_read[j] = m
                g, b = cols[:, 2 * which, k:k + 1], cols[:, 2 * which + 1, k:k + 1]
                hi, lo = (hT[:, w, k, c * BANK:(c + 1) * BANK] for w in range(2))
                h = put("scalar", lambda e, g=g, b=b, hi=hi, bank=bank: e.activation(
                    hi, banks[bank], ACT.Identity, bias=b, scale=g), (m, cols_in, *hT_free), "hT_hi")
                f = put("vector", lambda e, g=g, b=b, bank=bank: e.tensor_scalar(
                    banks[bank], banks[bank], g, b, ALU.mult, ALU.add), (h, m, cols_in), "hT_lo")
                t = put("vector", lambda e, hi=hi, lo=lo, bank=bank: e.tensor_tensor(
                    lo, banks[bank], hi.bitcast(F32), ALU.subtract), (f, *hT_free), "hT_lo")
                freed[bank] = (t,)
                done += [h, t]
            return done

        def rows_of(b, c, mv, rs):
            return [(xres[:, b % 2, t, :], mv[:, t, 0:1], rs[:, t:t + 1]) for t in range(c * TPC, (c + 1) * TPC)]

        TERMS = ((0, 0), (0, 1), (1, 0))

        def context():
            for a in range(2):
                bpt = PART // M
                for k, rows_k in ((0, PART), (1, CREST)):
                    bank = f"T{k}"
                    m = put("tensor", lambda e, a=a, k=k, rows_k=rows_k, bank=bank: e.transpose(
                        banks[bank][0:rows_k, 0:PART], ctx_sb[:, a, k * PART:k * PART + rows_k], ident[:, :]),
                        (ctx_in, ident_in, *freed[bank]), "ctx_turned")
                    ctxT_in = put("vector", lambda e, a=a, k=k, rows_k=rows_k, bank=bank, bpt=bpt: e.tensor_copy(
                        ctxT[0:rows_k, k, a * bpt:(a + 1) * bpt, :],
                        banks[bank][0:rows_k, 0:PART].rearrange("p (b m) -> p b m", b=bpt)), (m,), "ctx_copied")
                    freed[bank] = (ctxT_in,)
            order = ["S0a", "S0b", "S1a", "S1b", "PV", "PJ"]
            n = 0
            diag_in = {}
            for i in range(2):
                for p in range(PAIRS):
                    bank = order[n % 6]
                    n += 1

                    def product(e, i=i, p=p, bank=bank):
                        for k, rows_k in ((0, PART), (1, CREST)):
                            last = e.matmul(banks[bank][:, 0:B * M], wkv2[0:rows_k, i, k, p * PART:(p + 1) * PART],
                                            ctxT[0:rows_k, k, :, :], start=(k == 0), stop=(k == 1))
                        return last
                    m = put("tensor", product, (ctxT_in, wkv2_in, *freed[bank]), "ctx_product")
                    done = []
                    for half, engine in ((0, "vector"), (1, "scalar")):
                        r = slice(half * DH, (half + 1) * DH)
                        src = banks[bank][r, 0:B * M].rearrange("p (b m) -> p b m", b=B)
                        dst = diag[r, i, :, p, r]
                        f = (lambda e, dst=dst, src=src: e.tensor_copy(dst, src)) if engine == "vector" else \
                            (lambda e, dst=dst, src=src: e.copy(dst, src))
                        done.append(put(engine, f, (m, zero_a, zero_b), f"diag_{engine}"))
                    freed[bank] = diag_in[i, p] = tuple(done)
            for k in range(KT):
                for h in range(PAIRS // 4):
                    bank = f"T{(2 * k + h) % 2}"

                    def product(e, k=k, h=h, bank=bank):
                        for j in range(4):
                            p = 4 * h + j
                            last = e.transpose(banks[bank][:, j * PART:(j + 1) * PART],
                                               wq2[:, k, p * PART:(p + 1) * PART], ident[:, :])
                        return last
                    m = put("tensor", product, (wq2_in, *freed[bank]), "wq2_turned")
                    dst = wq2T[:, 4 * h:4 * h + 4, k * PART:(k + 1) * PART]
                    src = banks[bank].rearrange("p (j n) -> p j n", j=4)
                    wq2T_in = put("scalar", lambda e, dst=dst, src=src: e.copy(dst, src), (m,), "wq2T_in")
                    freed[bank] = (wq2T_in,)
            for p in range(PAIRS):
                for k in range(KT):
                    bank = order[n % 6]
                    n += 1
                    m = put("tensor", lambda e, p=p, k=k, bank=bank: e.matmul(
                        banks[bank], wq2T[:, p, k * PART:(k + 1) * PART], diag[:, 0, :, p, :],
                        start=True, stop=True), (wq2T_in, *diag_in[0, p], *freed[bank]), "keys2_product")
                    dst = keys2[:, :, k, p * PART:(p + 1) * PART]
                    src = banks[bank].rearrange("p (b n) -> p b n", b=B)
                    if n % 2:
                        t = put("scalar", lambda e, dst=dst, src=src: e.activation(dst, src, ACT.Copy, scale=SCALE),
                                (m,), "keys2_act")
                        t_act = t
                    else:
                        t = put("vector", lambda e, dst=dst, src=src: e.tensor_scalar(dst, src, SCALE, None, ALU.mult),
                                (m,), "keys2_dve")
                        t_dve = t
                    freed[bank] = (t,)
            keys_last = m
            stored = dma(lambda e: e.dma_start(cross_dram[:, :, 0].rearrange("b p n -> p b n"),
                                      keys2[:, :, :, :].rearrange("p b k n -> p b (k n)")),
                (t_act, t_dve), "keys2_stored")
            qk_free[0] = keys2_stored[0] = stored
            for b in range(B):
                for p in range(PAIRS):
                    bank = order[n % 6]
                    n += 1
                    m = put("tensor", lambda e, b=b, p=p, bank=bank: e.matmul(
                        banks[bank][:, 0:DIM], diag[:, 1, b, p, :], wo2[:, p, :], start=True, stop=True),
                        (wo2_in, *diag_in[1, p], *freed[bank]), "values2_product")
                    dst = values2[:, b, p, :]
                    if n % 2:
                        t = t_act = put("scalar", lambda e, dst=dst, bank=bank: e.copy(dst, banks[bank][:, 0:DIM]),
                                        (m, keys_last), "values2_act")
                    else:
                        t = t_dve = put("vector", lambda e, dst=dst, bank=bank: e.tensor_copy(
                            dst, banks[bank][:, 0:DIM]), (m, keys_last), "values2_dve")
                    freed[bank] = (t,)
            stored = dma(lambda e: e.dma_start(cross_dram[:, :, 1].rearrange("b p n -> p b n"),
                                               values2[:, :, :, :].rearrange("p b q n -> p b (q n)")),
                         (t_act, t_dve), "values2_stored")
            return stored

        q_ready, k_ready, v_ready, k_dup = {}, {}, {}, {}
        s_done, t_done, pv_part = {}, {}, {}
        qk_free, keys2_stored, oT_free, probs_free = [None], [None], [], [None]

        def project_qk(P, kind, c, h_ready):
            par = P % 2

            def product(e):
                for i, (w, h) in enumerate(TERMS):
                    for k in range(KT):
                        last = e.matmul(PJ[:, :], wqk[:, par, w, kind, k, :], hT[:, h, k, c * BANK:(c + 1) * BANK],
                                        start=(i == k == 0), stop=(i == 2 and k == KT - 1))
                return last
            m = put("tensor", product, (wqk_in[P], *h_ready, *freed["PJ"]), "projected")
            span = slice(c * BANK, (c + 1) * BANK)
            halves = []
            for head in range(2):
                r = slice(head * DH, (head + 1) * DH)
                o = slice((1 - head) * DH, (2 - head) * DH)
                hi = qk[r, par, head, 0 if kind == 0 else 1, span]
                lo = qk[o, par, head, 0, span] if kind == 0 else qk[r, par, head, 2, span]
                scale = SCALE if kind == 0 else 1.0
                a = put("scalar", lambda e, hi=hi, r=r, scale=scale: e.activation(
                    hi, PJ[r, :], ACT.Copy, scale=scale),
                    (m, s_done.get(f"pair{P - 2}"), k_dup.get(P - 2), qk_free[0]), "split_hi")
                halves.append((r, hi, lo, scale, a))
            for r, hi, lo, scale, a in halves:
                d = put("vector", lambda e, r=r, hi=hi, lo=lo, scale=scale: e.scalar_tensor_tensor(
                    lo, PJ[r, :], scale, hi.bitcast(F32), ALU.mult, ALU.subtract), (a,), "split_lo")
            freed["PJ"] = (d,)
            (q_ready if kind == 0 else k_ready)[P] = (a, d)
            qk_done[P] = m

        def duplicate_k(P):
            for head in range(2):
                r, o = slice(head * DH, (head + 1) * DH), slice((1 - head) * DH, (2 - head) * DH)
                t = dma(lambda e, head=head, r=r, o=o: e.dma_start(
                    qk[o, P % 2, head, 1:3, :].bitcast(F32), qk[r, P % 2, head, 1:3, :].bitcast(F32)),
                    k_ready[P], f"k_doubled{P % 2}")
            k_dup[P] = t

        def project_v(D, u, h_ready):
            def product(e):
                for j in range(2):
                    t = 2 * u + j
                    for i, (h, w) in enumerate(TERMS):
                        for k in range(KT):
                            last = e.matmul(PJ[:, j * DIM:j * DIM + 2 * PART], hT[:, h, k, t * PART:(t + 1) * PART],
                                            wv[:, w, k, :], start=(i == k == 0), stop=(i == 2 and k == KT - 1))
                return last
            m = put("tensor", product, (wv_in[D], *h_ready, *freed["PJ"]), "projected")
            dst = v_sb[:, 2 * u:2 * u + 2, :].rearrange("p t n -> p (t n)")
            v_ready[D, u] = put("scalar", lambda e: e.copy(dst, PJ[:, 0:4 * PART]), (m, pv_part.get((D, u))), "v_copied")
            freed["PJ"] = (v_ready[D, u],)
            v_done[D] = m

        norm_done, exp_done, max_done, pT_written, o_written = {}, {}, {}, {}, {}

        def score(n):
            P, it, head = n // (2 * TILES), n // 2 % TILES, n % 2
            a = f"S{n % 2}a", f"S{n % 2}b"

            def product(e):
                q = qk[:, P % 2, head, 0, it * PART:(it + 1) * PART]
                for half in range(2):
                    for part in (1, 2):
                        last = e.matmul(SC[n % 2][:, half * BANK:(half + 1) * BANK], q,
                                        qk[:, P % 2, head, part, half * BANK:(half + 1) * BANK],
                                        start=(part == 1), stop=(part == 2))
                return last
            s_done[n] = put("tensor", product, (*q_ready[P], *k_ready[P], k_dup[P], *freed[a[0]], *freed[a[1]]),
                            "scored")
            if it == TILES - 1 and head == 1:
                s_done[f"pair{P}"] = s_done[n]

        def row_max(n):
            max_done[n] = put("vector", lambda e: e.tensor_reduce(
                nmax[:, n % 8:n % 8 + 1], SC[n % 2][:, :], AX.X, ALU.max, negate=True), (s_done[n],), "row_max")

        def exponential(n):
            exp_done[n] = put("scalar", lambda e: e.activation(
                probs[:, n % 3, :], SC[n % 2][:, :], ACT.Exp, bias=nmax[:, n % 8:n % 8 + 1],
                accum_out=lsum[:, n % 8:n % 8 + 1]), (max_done[n], t_done.get(n - 3), probs_free[0]), "exponential")
            freed[f"S{n % 2}a"] = freed[f"S{n % 2}b"] = (exp_done[n],)

        def normalise(n):
            t = put("vector", lambda e: e.reciprocal(rsum[:, n % 8:n % 8 + 1], lsum[:, n % 8:n % 8 + 1]),
                    (exp_done[n],), "row_sum")
            norm_done[n] = put("gpsimd", lambda e: e.tensor_scalar(
                probs[:, n % 3, :], probs[:, n % 3, :], rsum[:, n % 8:n % 8 + 1], 1.0, ALU.mult, ALU.mult),
                (t, exp_done[n]), "normalised")

        def turn(n):
            g, it, head = n // 4, n // 2 % 2, n % 2
            for half in range(2):
                bank = f"T{half}"

                def product(e, half=half, bank=bank):
                    for j in range(4):
                        jt = half * 4 + j
                        last = e.transpose(banks[bank][:, j * PART:(j + 1) * PART],
                                           probs[:, n % 3, jt * PART:(jt + 1) * PART], ident[:, :])
                    return last
                t_done[n] = put("tensor", product, (norm_done[n], *freed[bank]), "turned_p")
                dst = pT[:, g % 2, head, half * 4:half * 4 + 4, it * PART:(it + 1) * PART]
                src = banks[bank].rearrange("p (j n) -> p j n", j=4)
                waits = (t_done[n], pv_part.get(("group", g - 2)))
                if half == 0:
                    t = put("scalar", lambda e, dst=dst, src=src: e.copy(dst, src), waits, "pT_act")
                else:
                    t = put("vector", lambda e, dst=dst, src=src: e.tensor_copy(dst, src), waits, "pT_dve")
                freed[bank] = (t,)
                pT_written[n, half] = t

        def attend(g, part):
            P = g * 4 // (2 * TILES)

            def product(e):
                for jt in (2 * part, 2 * part + 1):
                    for head in range(2):
                        r = slice(head * DH, (head + 1) * DH)
                        c0 = (P % 2) * PART + head * DH
                        last = e.matmul(PV[r, 0:2 * PART], v_sb[:, jt, c0:c0 + DH], pT[:, g % 2, head, jt, :],
                                        start=(jt == 0), stop=(jt == TILES - 1))
                return last
            waits = [v_ready[P // 2, part], *freed["PV"]]
            waits += [pT_written[4 * g + i, h] for i in range(4) for h in range(2)]
            t = put("tensor", product, waits, "attended")
            pv_part[P // 2 + 1, part] = t
            if part == 3:
                pv_part["group", g] = t
                i0 = (g * 2 % TILES) * PART
                o_written[P] = put("scalar", lambda e: e.copy(oT[:, P % PAIRS, i0:i0 + 2 * PART],
                                                              PV[:, 0:2 * PART]),
                                   (t, *oT_free), "oT_written")
                freed["PV"] = (o_written[P],)

        steps = PAIRS * 2 * TILES

        def self_attention(b, h_ready):
            P0, n0, W = b * PAIRS, b * steps, 2 * TILES
            for i in range(steps + 10):
                n, p, s = n0 + i, i // W, i % W
                if i < steps:
                    score(n)
                if 0 <= i - 1 < steps:
                    normalise(n - 1)
                if i < steps:
                    row_max(n)
                if 0 <= i - 2 < steps:
                    turn(n - 2)
                if i < steps:
                    exponential(n)
                j = i - 6
                if 0 <= j < steps:
                    attend((n0 + j) // 4, j % 4)
                if i >= steps:
                    continue
                P = P0 + p
                if p % 2 == 0 and 3 <= s < 7:
                    project_v(P // 2, s - 3, h_ready)
                if s in (7, 9, 11, 13) and p + 1 < PAIRS:
                    u = (s - 7) // 2
                    project_qk(P + 1, 1 if u < 2 else 0, u % 2, h_ready)
                    if u == 1:
                        duplicate_k(P + 1)
                if s == 8 and p % 2 == 0 and P // 2 + 1 < B * PAIRS // 2:
                    stream_v(P // 2 + 1)
                if s == 14 and P + 2 < B * PAIRS:
                    stream_qk(P + 2)

        ring_read = {}
        bias_added = {}

        def output(b, t, slot, ready, w, name):
            bank = ("PV", "PJ")[t % 2]

            def product(e):
                for i, (o, h) in enumerate(TERMS):
                    for p in range(PAIRS):
                        last = e.matmul(banks[bank][:, 0:DIM], turned[:, slot, o, p, :], w[:, h, p, :],
                                        start=(i == p == 0), stop=(i == 2 and p == PAIRS - 1))
                return last
            m = put("tensor", product, (*ready, *freed[bank]), "out_product")
            ring_read[slot] = m
            added = put("vector", lambda e: e.tensor_tensor(
                xres[:, b % 2, t, :], banks[bank][:, 0:DIM], xres[:, b % 2, t, :], ALU.add),
                (m, bias_added[b, t]), name)
            freed[bank] = (added,)
            return m, added

        def add_bias(b, i, tiles, waits):
            for t in tiles:
                bias_added[b, t] = put("gpsimd", lambda e, t=t: e.tensor_tensor(
                    xres[:, b % 2, t, :], xres[:, b % 2, t, :], rows[:, i, :], ALU.add),
                    (*waits, rows_in), "bias_added")

        out_count = [0]

        def turned_output1(b, t, scores_over):
            slot = out_count[0] % 3
            out_count[0] += 1
            hi, lo = turned[:, slot, 0], turned[:, slot, 1]
            src = oT[:, :, t * PART:(t + 1) * PART]
            h = put("scalar", lambda e: e.copy(hi, src), (o_written[b * PAIRS + PAIRS - 1], ring_read.get(slot),
                                                          scores_over), "oT_hi")
            lo_t = put("vector", lambda e: e.tensor_tensor(lo, src, hi.bitcast(F32), ALU.subtract),
                       (h, ring_read.get(slot), scores_over), "oT_lo")
            oT_free[:] = [h, lo_t]
            return output(b, t, slot, (h, lo_t, wo1_in), wo1, "x1_added")

        def cross_attention(b, h_ready, cross_in, hooks):
            sub_done, exp2, sum2, scaled2, turned_ready, p2_read = {}, {}, {}, {}, {}, {}
            x_done = {}

            def score2(t):
                c = t // TPC

                def product(e):
                    for half in range(2):
                        for i, (h, w) in enumerate(TERMS):
                            for k in range(KT):
                                last = e.matmul(SC[t % 2][:, half * BANK:(half + 1) * BANK],
                                                hT[:, h, k, t * PART:(t + 1) * PART],
                                                keys_hl[:, w, k, half * BANK:(half + 1) * BANK],
                                                start=(i == k == 0), stop=(i == 2 and k == KT - 1))
                    return last
                s = put("tensor", product, (*h_ready[c], *cross_in, *freed[f"S{t % 2}a"], *freed[f"S{t % 2}b"]),
                        "scored2")
                hT_read[0] = s
                s3 = SC[t % 2][:, :].rearrange("p (h m) -> p h m", h=HEADS)
                P3 = probs[:, t % 3, :].rearrange("p (h m) -> p h m", h=HEADS)
                nm = nmax2[:, t % 2, :]
                mx = put("vector", lambda e: e.tensor_reduce(nm, s3, AX.X, ALU.max, negate=True),
                         (s, sub_done.get(t - 2), soft2_last[0]), "soft2")
                sub = put("vector", lambda e: e.tensor_tensor(
                    P3, s3, nm.unsqueeze(2).to_broadcast([PART, HEADS, M]), ALU.add),
                    (mx, p2_read.get(t - 3)), "soft2")
                sub_done[t] = soft2_last[0] = sub
                freed[f"S{t % 2}a"] = freed[f"S{t % 2}b"] = (sub,)
                exp2[t] = put("scalar", lambda e: e.activation(probs[:, t % 3, :], probs[:, t % 3, :], ACT.Exp),
                              (sub,), "exp2")

            def soften2(t):
                P3 = probs[:, t % 3, :].rearrange("p (h m) -> p h m", h=HEADS)
                ls, rr = lsum2[:, t % 2, :], rsum2[:, t % 2, :]
                su = put("vector", lambda e: e.tensor_reduce(ls, P3, AX.X, ALU.add), (exp2[t], soft2_last[0]),
                         "soft2")
                rc = put("vector", lambda e: e.reciprocal(rr, ls), (su, scaled2.get(t - 2)), "soft2")
                soft2_last[0] = rc
                scaled2[t] = put("gpsimd", lambda e: e.tensor_tensor(
                    P3, P3, rr.unsqueeze(2).to_broadcast([PART, HEADS, M]), ALU.mult), (rc,), "scaled2")

            def turn2(t):
                slot = out_count[0] % 3
                out_count[0] += 1
                turned_ready[t] = (slot,)
                for half in range(2):
                    bank = f"T{half}"

                    def product(e, half=half, bank=bank):
                        for j in range(4):
                            p = half * 4 + j
                            last = e.transpose(banks[bank][:, j * PART:(j + 1) * PART],
                                               probs[:, t % 3, p * PART:(p + 1) * PART], ident[:, :])
                        return last
                    m = put("tensor", product, (scaled2[t], *freed[bank]), "turned2")
                    p2_read[t] = probs_free[0] = m
                    hi, lo = (turned[:, slot, w, half * 4:half * 4 + 4, :].rearrange("p j n -> p (j n)")
                              for w in range(2))
                    h = put("scalar", lambda e, hi=hi, bank=bank: e.copy(hi, banks[bank]),
                            (m, ring_read.get(slot)), "p2T_hi")
                    d = put("vector", lambda e, hi=hi, lo=lo, bank=bank: e.tensor_tensor(
                        lo, banks[bank], hi.bitcast(F32), ALU.subtract), (h, ring_read.get(slot)), "p2T_lo")
                    freed[bank] = (d,)
                    turned_ready[t] += (h, d)

            def out2(t):
                slot, *ready = turned_ready[t]
                out_done[0], x_done[t] = output(b, t, slot, (*ready, *cross_in), values_hl, "x2_added")
                ln3_done[b] = ln_stats(xres[:, b % 2, t, :], mv3[:, b, t, :], t, x_done[t])

            for i in range(TILES + 3):
                if 0 <= i - 1 < TILES:
                    soften2(i - 1)
                if i < TILES:
                    score2(i)
                if 0 <= i - 2 < TILES:
                    turn2(i - 2)
                if 0 <= i - 3 < TILES:
                    out2(i - 3)
                if i in hooks:
                    hooks[i]()
            return x_done

        soft2_last, hT_read, out_done = [None], [None], [None]
        ln3_done = {}

        x_stored, h1_ready = {}, {}

        def stats1(b):
            for t in range(TILES):
                agg = ln_stats(xres[:, b % 2, t, :], mv1[:, t, :], t, x_in[b])
            rstd1[b] = ln_rstd(mv1[:, :, 1], rs1[:, :], (agg, ln1_read[0]))

        rstd1, ln1_read = {}, [None]

        def norm1(b, c):
            ready = ln_rows(rows_of(b, c, mv1, rs1), (rstd1[b],))
            ln1_read[0] = ready
            h1_ready[b, c] = ln_turn(c, ready, 0, (hT_read[0],))
            add_bias(b, 0, range(c * TPC, (c + 1) * TPC), (ready,))

        stats1(0)
        for c in range(CHUNKS):
            norm1(0, c)
        values2_stored = context()
        oT_free[:] = [values2_stored]
        for b in range(B):
            P0 = b * PAIRS
            h_all = [t for c in range(CHUNKS) for t in h1_ready[b, c]]
            for u in range(4):
                project_qk(P0, 1 if u < 2 else 0, u % 2, h_all)
                if u == 1:
                    duplicate_k(P0)
            if b + 1 < B:
                x_in[b + 1] = load_x(b + 1, (x_stored.get(b - 1, wo1_in), ln3_done.get(b - 1)))
            self_attention(b, h_all)
            scores_over, group_over = s_done[f"pair{P0 + PAIRS - 1}"], pv_part["group", (b + 1) * steps // 4 - 1]

            def split_cross(i, b=b, scores_over=scores_over, group_over=group_over):
                raw = dma(lambda e: e.dma_start(raw_cross[:, i], cross_dram[b, :, i]),
                          (scores_over, keys2_stored[0], values2_stored), f"raw_cross_loaded{i}")
                hi, lo = cross[:, i, 0], cross[:, i, 1]

                def split():
                    if i:
                        return (split_weights(raw_cross[:, i], hi, lo, raw, group_over, "cross_split"),)
                    h = put("scalar", lambda e: e.copy(hi, raw_cross[:, i]), (raw, group_over), "cross_hi")
                    return h, put("vector", lambda e: e.tensor_tensor(lo, raw_cross[:, i], hi.bitcast(F32),
                                                                      ALU.subtract), (h,), "cross_lo")
                return split
            split_keys, split_values = split_cross(0), split_cross(1)

            x1, h2_ready = {}, {}
            ln2 = {}

            def norm2(c, b=b):
                ln2[c] = ln_rows(rows_of(b, c, mv2, rs2), (r2,))
                add_bias(b, 1, range(c * TPC, (c + 1) * TPC), (ln2[c],))

            for t in range(TILES):
                m, x1[t] = turned_output1(b, t, scores_over)
                agg = ln_stats(xres[:, b % 2, t, :], mv2[:, t, :], t, x1[t])
                if t % TPC == TPC - 1:
                    r2 = ln_rstd(mv2[:, t - TPC + 1:t + 1, 1], rs2[:, t - TPC + 1:t + 1], (agg,))
                if t == TPC:
                    norm2(0)
                if t == TPC + 1:
                    hT_free = (qk_done[P0 + PAIRS - 1], v_done[(P0 + PAIRS - 1) // 2])
                    h2_ready[0] = ln_turn(0, ln2[0], 1, hT_free)
                    keys_in = split_keys()
                    values_in = split_values()
            norm2(1)
            raw_ffn_in = {}
            if b == B - 1:
                dma(lambda e: e.dma_start(raw_wp[:, :, :], Wp.rearrange("(k p) n -> p k n", p=PART)),
                    tuple(oT_free), "ffn_loaded")
                ffn_raw = dma(lambda e: e.dma_start(raw_w2[:, :, :], W2.rearrange("(f p) n -> p f n", p=PART)),
                              tuple(oT_free), "ffn_loaded")

            def turn_chunk1(hT_free=hT_free, h2_ready=h2_ready, ln2=ln2):
                h2_ready[1] = ln_turn(1, ln2[1], 1, hT_free)

            hooks = {1: turn_chunk1}
            if b + 1 < B:
                hooks[3] = lambda b=b: stats1(b + 1)
                hooks[TILES - 1] = lambda b=b: norm1(b + 1, 0)
                hooks[TILES + 1] = lambda b=b: norm1(b + 1, 1)
            x_done = cross_attention(b, h2_ready, (*keys_in, *values_in), hooks)
            x_stored[b] = dma(lambda e, b=b: e.dma_start(xmid[b], xres[:, b % 2]), (x_done[TILES - 1],),
                              f"x_stored{b % 2}")

        NCH = B * CHUNKS
        cross_over = out_done[0]
        r3 = ln_rstd(mv3[:, :, :, 1].rearrange("p b t -> p (b t)"), rs3[:, :], (ln3_done[B - 1],))
        xf_in, biased, h3, u_ready, up_read, down_read, gate_read, u_read, stored = ({} for _ in range(9))
        wp_in = {}

        def split_ffn(q):
            n = FF // 4
            wide = lambda w: w.rearrange("p k (g n) -> p k g n", g=2)[:, :, :, q * n:(q + 1) * n]
            f4 = FT // 4
            tickets = ()
            for raw, hi, lo in ((wide(raw_wp[:, :, :]), wide(wp[:, 0]), wide(wp[:, 1])),
                                (raw_w2[:, q * f4:(q + 1) * f4], w2[:, 0, q * f4:(q + 1) * f4],
                                 w2[:, 1, q * f4:(q + 1) * f4])):
                h = put("scalar", lambda e, hi=hi, raw=raw: e.copy(hi, raw), (ffn_raw, cross_over), "ffn_hi")
                tickets += (h, put("vector", lambda e, hi=hi, lo=lo, raw=raw: e.tensor_tensor(
                    lo, raw, hi.bitcast(F32), ALU.subtract), (h,), "ffn_lo"))
            wp_in[q] = tickets

        def load_chunk(c):
            b, t0 = c // CHUNKS, (c % CHUNKS) * TPC
            xf_in[c] = dma(lambda e: e.dma_start(xf[:, c % 4], xmid[b, :, t0:t0 + TPC, :]),
                           (x_stored[b], x_stored[B - 2], x_stored[B - 1] if c > 1 else None,
                            ln3_done[B - 2], ln3_done[B - 1] if c > 1 else None, stored.get(c - 4),
                            xf_in.get(c - 4)), f"xf_loaded{c % 4}")

        def chunk_rows(c):
            b, t0 = c // CHUNKS, (c % CHUNKS) * TPC
            tiles = [(xf[:, c % 4, j, :], mv3[:, b, t0 + j, 0:1],
                      rs3[:, b * TILES + t0 + j:b * TILES + t0 + j + 1]) for j in range(TPC)]
            ready = ln_rows(tiles, (r3, xf_in[c]))
            biased[c] = put("gpsimd", lambda e: e.tensor_tensor(
                xf[:, c % 4], xf[:, c % 4], rows[:, 2:3, :].to_broadcast([PART, TPC, DIM]), ALU.add),
                (ready, rows_in), "bias3_added")
            return ready

        def chunk_turn(c, ready):
            h3[c] = ln_turn(c % 2, ready, 2, (up_read.get(c - 2, hT_read[0]),))

        def ffn_up(c, f):
            i = c * FT + f
            for which, bank in ((1, ("S0a", "S1a")[f % 2]), (0, ("S0b", "S1b")[f % 2])):
                col = which * FT + f

                def product(e, col=col, bank=bank):
                    for i, (w, h) in enumerate(TERMS):
                        for k in range(KT):
                            last = e.matmul(banks[bank], wp[:, w, k, col * PART:(col + 1) * PART],
                                            hT[:, h, k, (c % 2) * BANK:(c % 2 + 1) * BANK],
                                            start=(i == k == 0), stop=(i == 2 and k == KT - 1))
                    return last
                m = put("tensor", product, (*h3[c], *wp_in[f * 4 // FT], *freed[bank]), "up_product")
                if which == 1:
                    g = put("scalar", lambda e, bank=bank, col=col: e.activation(
                        gate[:, i % 4, :], banks[bank], ACT.Gelu, bias=bp_col[:, col:col + 1]),
                        (m, bp_in, gate_read.get(i - 4)), "gelu")
                    freed[bank] = (g,)
                else:
                    u = put("vector", lambda e, bank=bank, col=col: e.scalar_tensor_tensor(
                        u_full[:, i % 3, :], banks[bank], bp_col[:, col:col + 1], gate[:, i % 4, :],
                        ALU.add, ALU.mult), (m, g, u_read.get(i - 3)), "gated")
                    freed[bank] = (u,)
                    gate_read[i] = u
            hi, lo = uT[:, c % 2, 0, f, :], uT[:, c % 2, 1, f, :]
            free = down_read.get(c - 2)
            h = put("scalar", lambda e: e.copy(hi, u_full[:, i % 3, :]), (u, free), "u_hi")
            u_read[i] = put("vector", lambda e: e.tensor_tensor(lo, u_full[:, i % 3, :], hi.bitcast(F32),
                                                                ALU.subtract), (h, free), "u_lo")
            u_ready[c] = (h, u_read[i])
            up_read[c] = m

        def ffn_down(c, j):
            b, t0 = c // CHUNKS, (c % CHUNKS) * TPC
            bank = ("PV", "PJ")[j % 2]

            def product(e):
                for i, (o, h) in enumerate(TERMS):
                    for f in range(FT):
                        last = e.matmul(banks[bank][:, 0:DIM], uT[:, c % 2, o, f, j * PART:(j + 1) * PART],
                                        w2[:, h, f, :], start=(i == f == 0), stop=(i == 2 and f == FT - 1))
                return last
            m = put("tensor", product, (*u_ready[c], *wp_in[3], *freed[bank]), "down_product")
            down_read[c] = m
            y = put("vector", lambda e: e.tensor_tensor(xf[:, c % 4, j, :], banks[bank][:, 0:DIM],
                                                        xf[:, c % 4, j, :], ALU.add), (m, biased[c]), "y_added")
            freed[bank] = (y,)
            if j == TPC - 1:
                dst = out[b, t0 * PART:(t0 + TPC) * PART, :].rearrange("(t p) d -> p t d", p=PART)
                stored[c] = dma(lambda e: e.dma_start(dst, xf[:, c % 4]), (y,), f"y_stored{c % 2}")

        for c in range(4):
            load_chunk(c)
        split_ffn(0)
        rows_ready = chunk_rows(0)
        chunk_turn(0, rows_ready)
        for c in range(NCH + 1):
            for f in range(FT):
                if c < NCH:
                    ffn_up(c, f)
                    if c == 0 and f % 2 == 0 and f < 6:
                        split_ffn(f // 2 + 1)
                if f == 3 and c + 1 < NCH:
                    rows_ready = chunk_rows(c + 1)
                if f == 5 and c + 1 < NCH:
                    chunk_turn(c + 1, rows_ready)
                if c and f % 2 == 1:
                    ffn_down(c - 1, f // 2)
            if c and c + 3 < NCH:
                load_chunk(c + 3)

        block = stack.enter_context(nc.Block())

        @block.tensor
        def _(e):
            Q.play("tensor", e)

        @block.vector
        def _(e):
            Q.play("vector", e)

        @block.scalar
        def _(e):
            Q.play("scalar", e)

        @block.gpsimd
        def _(e):
            Q.play("gpsimd", e)

        @block.sync
        def _(e):
            Q.play("sync", e)
            for name in ("keys2_stored", "values2_stored", "x_stored0", "x_stored1", "y_stored0", "y_stored1"):
                e.wait_ge(semaphore(name), Q.raised[name])


_NAMES = ["x", "ctx_768"] + ["L0_xattn_" + n for n in (
    "Wq1 Wk1 Wv1 Wo1 bo1 Wq2 Wk2 Wv2 Wo2 bo2 Wp bp W2 b2 g1 be1 g2 be2 g3 be3").split()]


def kernel(**inputs):
    import numpy as np
    import concourse.bacc as bacc
    from concourse import mybir as mb
    from concourse.bass_utils import run_bass_kernel_spmd

    nc = bacc.Bacc("TRN2", target_bir_lowering=False, num_devices=1)
    arrays, args = {}, []
    for name in _NAMES:
        a = np.ascontiguousarray(inputs[name])
        arrays[f"in_{name}"] = a
        args.append(nc.dram_tensor(f"in_{name}", a.shape, mb.dt.from_np(a.dtype), kind="ExternalInput").ap())
    shape = inputs["x"].shape
    args.append(nc.dram_tensor("out_x", shape, mb.dt.float32, kind="ExternalOutput").ap())
    block_kernel(nc, *args)
    r = run_bass_kernel_spmd(nc, [arrays], core_ids=[0])
    return r.results[0]["out_x"]
```

```python
from contextlib import ExitStack

import concourse.bass as bass
from concourse import mybir
from concourse.alu_op_type import AluOpType as ALU

F32 = mybir.dt.float32
F32R = mybir.dt.float32r
ACT = mybir.ActivationFunctionType
AX = mybir.AxisListType

PART = 128
BANK = 512
EPS = 1e-5


class Queues:

    def __init__(self, semaphore):
        self.semaphore = semaphore
        self.streams = {"tensor": [], "vector": [], "scalar": [], "gpsimd": [], "sync": []}
        self.raised = {}

    def put(self, engine, emit, waits=(), signal=None, step=1):
        ticket = None
        if signal is not None:
            self.raised[signal] = self.raised.get(signal, 0) + step
            ticket = (signal, self.raised[signal])
        self.streams[engine].append((emit, waits, signal, step))
        return ticket

    def dma(self, emit, waits=(), signal=None):
        return self.put("sync", emit, waits, signal, 16)

    def play(self, name, engine):
        seen = {}
        for emit, waits, signal, step in self.streams[name]:
            for ticket in waits:
                if ticket is not None and seen.get(ticket[0], 0) < ticket[1]:
                    engine.wait_ge(self.semaphore(ticket[0]), ticket[1])
                    seen[ticket[0]] = ticket[1]
            last = emit(engine)
            if signal is not None:
                last.then_inc(self.semaphore(signal), step)


def block_kernel(nc, x, ctx, Wq1, Wk1, Wv1, Wo1, bo1, Wq2, Wk2, Wv2, Wo2, bo2, Wp, bp, W2, b2,
                 g1, be1, g2, be2, g3, be3, out):
    B, N, DIM = x.shape
    M, CD = ctx.shape[1:]
    INNER = Wq1.shape[1]
    DH = 64
    HEADS = INNER // DH
    SCALE = DH ** -0.5
    FF = W2.shape[0]
    KT = DIM // PART
    PAIRS = HEADS // 2
    TILES = N // PART
    CHUNKS = N // BANK
    TPC = BANK // PART
    FT = FF // PART
    CREST = CD - PART

    stack = ExitStack()
    with stack:
        def sb(name, shape, dt=F32):
            return stack.enter_context(nc.sbuf_tensor(name, shape, dt))

        def ps(name, shape):
            return stack.enter_context(nc.psum_tensor(name, shape, F32))

        ident = sb("ident", [PART, PART])
        eps = sb("eps", [PART, 1])
        cols = sb("cols", [PART, 6, KT])
        bp_col = sb("bp_col", [PART, 2 * FT])
        rows = sb("rows", [PART, 3, DIM])
        xres = sb("xres", [PART, 2, TILES, DIM])
        hT = sb("hT", [PART, 2, KT, N], F32R)
        xn = sb("xn", [PART, TPC, DIM])
        stats = sb("stats", [PART, TILES, 6])
        mv1 = sb("mv1", [PART, TILES, 2])
        mv2 = sb("mv2", [PART, TILES, 2])
        mv3 = sb("mv3", [PART, B, TILES, 2])
        sd = sb("sd", [PART, TILES])
        rs1 = sb("rs1", [PART, TILES])
        rs2 = sb("rs2", [PART, TILES])
        rs3 = sb("rs3", [PART, B, TILES])
        nmax = sb("nmax", [PART, 8])
        lsum = sb("lsum", [PART, 8])
        rsum = sb("rsum", [PART, 8])
        nmax2 = sb("nmax2", [PART, 2, HEADS])
        lsum2 = sb("lsum2", [PART, 2, HEADS])
        rsum2 = sb("rsum2", [PART, 2, HEADS])

        def overlay(*specs):
            with ExitStack() as scope:
                return [scope.enter_context(nc.sbuf_tensor(n, [PART, *shape], dt)) for n, shape, dt in specs]

        (oT, pT, qk, probs, v_sb, raw_qk, wqk, raw_v, wv, wo1) = overlay(
            ("oT", [PAIRS, N], F32),
            ("pT", [2, 2, TILES, 2 * PART], F32),
            ("qk", [2, 2, 3, N], F32R),
            ("probs", [3, N], F32),
            ("v_sb", [TILES, 2 * PART], F32),
            ("raw_qk", [2, KT, PART], F32),
            ("wqk", [2, 2, 2, KT, PART], F32R),
            ("raw_v", [KT, 2 * PART], F32),
            ("wv", [2, KT, 2 * PART], F32R),
            ("wo1", [2, PAIRS, DIM], F32R))
        (wkv2, wq2, wq2T, diag, _, keys2, wo2, ctx_sb, ctxT) = overlay(
            ("wkv2", [2, 2, INNER], F32),
            ("wq2", [KT, INNER], F32),
            ("wq2T", [PAIRS, DIM], F32),
            ("diag", [2, B, PAIRS, PART], F32),
            ("qk_even", [2, 3, N], F32),
            ("keys2", [B, KT, INNER], F32),
            ("wo2", [PAIRS, DIM], F32),
            ("ctx_sb", [2, CD], F32),
            ("ctxT", [2, B, M], F32))
        (values2,) = overlay(("values2", [B, PAIRS, DIM], F32))
        (_, cross, turned1, turned2, raw_keys2, _, raw_values2) = overlay(
            ("oT_kept", [PAIRS, N], F32),
            ("cross", [2, 2, 2 * INNER], F32R),
            ("turned1", [3, 2, PAIRS, PART], F32R),
            ("turned2", [3, 2, PAIRS, PART], F32R),
            ("raw_keys2", [2 * INNER], F32),
            ("probs_end", [3 * N - 2 * INNER], F32),
            ("raw_values2", [2 * INNER], F32))
        keys_hl = cross[:, 0].rearrange("p w (k n) -> p w k n", k=KT)
        values_hl = cross[:, 1].rearrange("p w (q n) -> p w q n", q=PAIRS)
        QF = 2 * FF // 4
        (raw_wp, raw_w2, gate, uT0, wp0, wp1, wp2, wp3, uT1, w2, u_full) = overlay(
            ("raw_wp", [KT, 2 * FF], F32), ("raw_w2", [FT, DIM], F32), ("gate", [4, BANK], F32),
            ("uT0", [2, FT, BANK], F32R),
            *((f"wp{q}", [2, KT, 2, QF // 2], F32R) for q in range(4)),
            ("uT1", [2, FT, BANK], F32R), ("w2", [2, FT, DIM], F32R), ("u_full", [3, BANK], F32))
        uT, wp = (uT0, uT1), (wp0, wp1, wp2, wp3)
        xf = xres[:, :, :, :].rearrange("p a (c t) n -> p (a c) t n", t=TPC)

        SC = [ps(f"score{i}", [PART, 2 * BANK]) for i in range(2)]
        TP = [ps(f"turn{i}", [PART, BANK]) for i in range(2)]
        PV = ps("attn_out", [PART, BANK])
        PJ = ps("project", [PART, BANK])
        banks = {"S0a": SC[0][:, 0:BANK], "S0b": SC[0][:, BANK:], "S1a": SC[1][:, 0:BANK],
                 "S1b": SC[1][:, BANK:], "T0": TP[0][:, :], "T1": TP[1][:, :], "PV": PV[:, :], "PJ": PJ[:, :]}
        freed = {name: () for name in banks}

        cross_dram = nc.dram_tensor("cross_tiles", (B, PART, 2, 2 * INNER), F32, kind="Internal").ap()
        xmid = nc.dram_tensor("x_middle", (B, PART, TILES, DIM), F32, kind="Internal").ap()

        sems = {}

        def semaphore(name):
            if name not in sems:
                sems[name] = stack.enter_context(nc.semaphore(name))
            return sems[name]

        Q = Queues(semaphore)
        put, dma = Q.put, Q.dma

        def load_x(b, waits=()):
            return dma(lambda e: e.dma_start(xres[:, b % 2], x[b].rearrange("(t p) d -> p t d", p=PART)),
                       waits, f"x_loaded{b % 2}")

        raw_qk_read, raw_v_read = [None], [None]
        qk_done, v_done = {}, {}
        wqk_in, wv_in = {}, {}

        def split_weights(raw, hi, lo, loaded, buffer_free, name):
            h = put("gpsimd", lambda e: e.tensor_scalar(hi, raw, 1.0, 1.0, ALU.mult, ALU.mult),
                    (loaded, buffer_free), name)
            return put("gpsimd", lambda e: e.tensor_tensor(lo, raw, hi.bitcast(F32), ALU.subtract), (h,), name)

        def stream_qk(P):
            c = (P % PAIRS) * PART
            for i, w in enumerate((Wq1, Wk1)):
                src = w.rearrange("(k p) n -> p k n", p=PART)[:, :, c:c + PART]
                t = dma(lambda e, i=i, src=src: e.dma_start(raw_qk[:, i], src), (raw_qk_read[0],), "wqk_loaded")
            flat = "p i k n -> p (i k n)"
            raw_qk_read[0] = wqk_in[P] = split_weights(
                raw_qk[:, :, :, :].rearrange(flat), wqk[:, P % 2, 0].rearrange(flat),
                wqk[:, P % 2, 1].rearrange(flat), t, qk_done.get(P - 2), "wqk_split")

        def stream_v(D):
            c = (D % (PAIRS // 2)) * 2 * PART
            src = Wv1.rearrange("(k p) n -> p k n", p=PART)[:, :, c:c + 2 * PART]
            t = dma(lambda e: e.dma_start(raw_v[:, :, :], src), (raw_v_read[0],), "wv_loaded")
            flat = "p k n -> p (k n)"
            raw_v_read[0] = wv_in[D] = split_weights(
                raw_v[:, :, :].rearrange(flat), wv[:, 0].rearrange(flat), wv[:, 1].rearrange(flat), t,
                v_done.get(D - 1), "wv_split")

        x_in = {0: load_x(0)}
        for i, v in enumerate((g1, be1, g2, be2, g3, be3)):
            cols_in = dma(lambda e, i=i, v=v: e.dma_start(cols[:, i, :], v.rearrange("(k p) -> p k", p=PART),
                                                          allow_slow_non_contiguous=True), signal="cols_loaded")
        ctx_rows = ctx.rearrange("b m c -> (b m) c").rearrange("(a p) c -> p a c", p=PART)
        ctx_in = dma(lambda e: e.dma_start(ctx_sb[:, :, :], ctx_rows), signal="ctx_loaded")
        wkv2_in = []
        for i, w in enumerate((Wk2, Wv2)):
            dma(lambda e, i=i, w=w: e.dma_start(wkv2[:, i, 0], w[0:PART]), signal=f"wkv2_loaded{i}")
            wkv2_in.append(dma(lambda e, i=i, w=w: e.dma_start(wkv2[0:CREST, i, 1], w[PART:CD]),
                               signal=f"wkv2_loaded{i}"))
        t = put("gpsimd", lambda e: e.memset(ident[:, :], 0.0), signal="const")
        ident_in = put("gpsimd", lambda e: e.affine_select(
            out=ident[:, :], in_=ident[:, :], compare_op=ALU.not_equal, fill=1.0, base=0,
            pattern=[[-1, PART]], channel_multiplier=1), (t,), "const")
        eps_in = put("gpsimd", lambda e: e.memset(eps[:, :], EPS), signal="const")
        diag_flat = diag[:, :, :, :, :].rearrange("p w b q n -> p (w b q n)")
        half = 2 * B * PAIRS * PART // 2
        zero_a = put("gpsimd", lambda e: e.memset(diag_flat[:, 0:half], 0.0), signal="const")
        zero_b = put("vector", lambda e: e.memset(diag_flat[:, half:2 * half], 0.0), signal="const_dve")
        stream_qk(0)
        stream_v(0)
        wq2_in = dma(lambda e: e.dma_start(wq2[:, :, :], Wq2.rearrange("(k p) n -> p k n", p=PART)),
                     signal="wq2_loaded")
        wo2_in = dma(lambda e: e.dma_start(wo2[:, :, :], Wo2.rearrange("(q p) n -> p q n", p=PART)),
                     signal="wo2_loaded")
        stream_qk(1)
        raw_wo1 = xres[:, 1].rearrange("p t n -> p (t n)")
        wo1_raw_in = dma(lambda e: e.dma_start(raw_wo1.rearrange("p (q n) -> p q n", q=PAIRS),
                                               Wo1.rearrange("(q p) n -> p q n", p=PART)), signal="wo1_loaded")
        for i, v in enumerate((bo1, bo2, b2)):
            rows_in = dma(lambda e, i=i, v=v: e.dma_start(
                rows[:, i, :], v.rearrange("(a n) -> a n", a=1).to_broadcast([PART, DIM])), signal="rows_loaded")
        bp_in = dma(lambda e: e.dma_start(bp_col[:, :], bp.rearrange("(f p) -> p f", p=PART),
                                          allow_slow_non_contiguous=True), signal="bp_loaded")
        wo1_in = split_weights(raw_wo1, wo1[:, 0].rearrange("p q n -> p (q n)"),
                               wo1[:, 1].rearrange("p q n -> p (q n)"), wo1_raw_in, None, "wo1_split")

        stats_read = {}

        def ln_stats(src, mv_of, slot, ready):
            st = put("vector", lambda e: e.bn_stats(stats[:, slot, :], src), (ready, stats_read.get(slot)), "ln_stat")
            stats_read[slot] = put("vector", lambda e: e.bn_aggr(mv_of, stats[:, slot, :]), (st,), "ln_stat")
            return stats_read[slot]

        sd_read = [None]

        def ln_root(var, waits):
            n = var.shape[-1]
            return put("scalar", lambda e: e.activation(sd[:, 0:n], var, ACT.Sqrt, bias=eps[:, 0:1]),
                       (*waits, eps_in, sd_read[0]), "ln_root")

        def ln_inverse(rs, root):
            sd_read[0] = put("vector", lambda e: e.reciprocal(rs, sd[:, 0:rs.shape[-1]]), (root,), "ln_stat")
            return sd_read[0]

        def ln_rstd(var, rs, waits):
            return ln_inverse(rs, ln_root(var, waits))

        xn_read = {}

        def ln_rows(tiles, waits, engine="vector", slots=range(TPC)):
            for slot in slots:
                src, mean, r = tiles[slot]
                t = put(engine, lambda e, slot=slot, src=src, mean=mean, r=r: e.tensor_scalar(
                    xn[:, slot, :], src, mean, r, ALU.subtract, ALU.mult), (*waits, xn_read.get(slot)),
                    f"ln_rows_{engine}")
            return t

        def ln_turn(c, ready, which, hT_free, through=("T0", "T1"), defer=False):
            done, parts = [], []
            for k in range(KT):
                bank = through[k]

                def product(e, k=k, bank=bank):
                    for j in range(TPC):
                        last = e.transpose(banks[bank][:, j * PART:(j + 1) * PART],
                                           xn[:, j, k * PART:(k + 1) * PART], ident[:, :])
                    return last
                m = put("tensor", product, (ready, ident_in, *freed[bank]), "ln_turned")
                for j in range(TPC):
                    xn_read[j] = m
                g, b = cols[:, 2 * which, k:k + 1], cols[:, 2 * which + 1, k:k + 1]
                hi, lo = (hT[:, w, k, c * BANK:(c + 1) * BANK] for w in range(2))
                h = put("scalar", lambda e, g=g, b=b, hi=hi, bank=bank: e.activation(
                    hi, banks[bank], ACT.Identity, bias=b, scale=g), (m, cols_in, *hT_free), "hT_hi")
                if k % 2 and not defer:
                    f = put("vector", lambda e, g=g, b=b, bank=bank: e.tensor_scalar(
                        banks[bank], banks[bank], g, b, ALU.mult, ALU.add), (h, m, cols_in), "hT_lo")
                else:
                    f = put("scalar", lambda e, g=g, b=b, bank=bank: e.activation(
                        banks[bank], banks[bank], ACT.Identity, bias=b, scale=g), (h,), "hT_full")

                def low(hi=hi, lo=lo, bank=bank, f=f, h=h):
                    t = put("vector", lambda e: e.tensor_tensor(lo, banks[bank], hi.bitcast(F32), ALU.subtract),
                            (f, *hT_free), "hT_lo")
                    freed[bank] = (t,)
                    return [h, t]
                if defer:
                    parts.append(low)
                else:
                    done += low()
            return (lambda: [t for low in parts for t in low()]) if defer else done

        def rows_of(b, c, mv, rs):
            return [(xres[:, b % 2, t, :], mv[:, t, 0:1], rs[:, t:t + 1]) for t in range(c * TPC, (c + 1) * TPC)]

        TERMS = ((0, 0), (0, 1), (1, 0))

        ctx_order = ["S0a", "S0b", "S1a", "S1b", "PV", "PJ"]
        ctxT_ready, ctx_products, diag_in = [None], [0], {}

        def context_turn():
            for a in range(2):
                bpt = PART // M
                for k, rows_k in ((0, PART), (1, CREST)):
                    bank = f"T{k}"
                    m = put("tensor", lambda e, a=a, k=k, rows_k=rows_k, bank=bank: e.transpose(
                        banks[bank][0:rows_k, 0:PART], ctx_sb[:, a, k * PART:k * PART + rows_k], ident[:, :]),
                        (ctx_in, ident_in, *freed[bank]), "ctx_turned")
                    ctxT_in = put("vector", lambda e, a=a, k=k, rows_k=rows_k, bank=bank, bpt=bpt: e.tensor_copy(
                        ctxT[0:rows_k, k, a * bpt:(a + 1) * bpt, :],
                        banks[bank][0:rows_k, 0:PART].rearrange("p (b m) -> p b m", b=bpt)), (m,), "ctx_copied")
                    freed[bank] = (ctxT_in,)
            ctxT_ready[0] = ctxT_in

        def context_product(i):
            for p in range(PAIRS):
                bank = ctx_order[ctx_products[0] % 6]
                ctx_products[0] += 1

                def product(e, p=p, bank=bank):
                    for k, rows_k in ((0, PART), (1, CREST)):
                        last = e.matmul(banks[bank][:, 0:B * M], wkv2[0:rows_k, i, k, p * PART:(p + 1) * PART],
                                        ctxT[0:rows_k, k, :, :], start=(k == 0), stop=(k == 1))
                    return last
                m = put("tensor", product, (ctxT_ready[0], wkv2_in[i], *freed[bank]), "ctx_product")
                done = []
                for half, engine in ((0, "vector"), (1, "scalar")):
                    r = slice(half * DH, (half + 1) * DH)
                    src = banks[bank][r, 0:B * M].rearrange("p (b m) -> p b m", b=B)
                    dst = diag[r, i, :, p, r]
                    f = (lambda e, dst=dst, src=src: e.tensor_copy(dst, src)) if engine == "vector" else \
                        (lambda e, dst=dst, src=src: e.copy(dst, src))
                    done.append(put(engine, f, (m, zero_a, zero_b), f"diag_{engine}"))
                freed[bank] = diag_in[i, p] = tuple(done)

        def context_fold():
            order, n = ctx_order, ctx_products[0]
            for k in range(KT):
                for h in range(PAIRS // 4):
                    bank = f"T{(2 * k + h) % 2}"

                    def product(e, k=k, h=h, bank=bank):
                        for j in range(4):
                            p = 4 * h + j
                            last = e.transpose(banks[bank][:, j * PART:(j + 1) * PART],
                                               wq2[:, k, p * PART:(p + 1) * PART], ident[:, :])
                        return last
                    m = put("tensor", product, (wq2_in, *freed[bank]), "wq2_turned")
                    dst = wq2T[:, 4 * h:4 * h + 4, k * PART:(k + 1) * PART]
                    src = banks[bank].rearrange("p (j n) -> p j n", j=4)
                    wq2T_in = put("scalar", lambda e, dst=dst, src=src: e.copy(dst, src), (m,), "wq2T_in")
                    freed[bank] = (wq2T_in,)
            for p in range(PAIRS):
                for k in range(KT):
                    bank = order[n % 6]
                    n += 1
                    m = put("tensor", lambda e, p=p, k=k, bank=bank: e.matmul(
                        banks[bank], wq2T[:, p, k * PART:(k + 1) * PART], diag[:, 0, :, p, :],
                        start=True, stop=True), (wq2T_in, *diag_in[0, p], *freed[bank]), "keys2_product")
                    dst = keys2[:, :, k, p * PART:(p + 1) * PART]
                    src = banks[bank].rearrange("p (b n) -> p b n", b=B)
                    if n % 2:
                        t = put("scalar", lambda e, dst=dst, src=src: e.activation(dst, src, ACT.Copy, scale=SCALE),
                                (m,), "keys2_act")
                        t_act = t
                    else:
                        t = put("vector", lambda e, dst=dst, src=src: e.tensor_scalar(dst, src, SCALE, None, ALU.mult),
                                (m,), "keys2_dve")
                        t_dve = t
                    freed[bank] = (t,)
            keys_last = m
            stored = dma(lambda e: e.dma_start(cross_dram[:, :, 0].rearrange("b p n -> p b n"),
                                      keys2[:, :, :, :].rearrange("p b k n -> p b (k n)")),
                (t_act, t_dve), "keys2_stored")
            keys2_stored[0] = stored
            for b in range(B):
                for p in range(PAIRS):
                    bank = order[n % 6]
                    n += 1
                    m = put("tensor", lambda e, b=b, p=p, bank=bank: e.matmul(
                        banks[bank][:, 0:DIM], diag[:, 1, b, p, :], wo2[:, p, :], start=True, stop=True),
                        (wo2_in, *diag_in[1, p], *freed[bank]), "values2_product")
                    dst = values2[:, b, p, :]
                    if n % 2:
                        t = t_act = put("scalar", lambda e, dst=dst, bank=bank: e.copy(dst, banks[bank][:, 0:DIM]),
                                        (m, keys_last), "values2_act")
                    else:
                        t = t_dve = put("vector", lambda e, dst=dst, bank=bank: e.tensor_copy(
                            dst, banks[bank][:, 0:DIM]), (m, keys_last), "values2_dve")
                    freed[bank] = (t,)
            stored = dma(lambda e: e.dma_start(cross_dram[:, :, 1].rearrange("b p n -> p b n"),
                                               values2[:, :, :, :].rearrange("p b q n -> p b (q n)")),
                         (t_act, t_dve), "values2_stored")
            return stored

        q_ready, k_ready, v_ready, k_dup = {}, {}, {}, {}
        s_done, t_done, pv_part = {}, {}, {}
        keys2_stored, oT_free, probs_free = [None], [], [None]

        def project_qk(P, kind, c, h_ready, bank="PJ"):
            par = P % 2

            def product(e):
                for i, (w, h) in enumerate(TERMS):
                    for k in range(KT):
                        last = e.matmul(banks[bank], wqk[:, par, w, kind, k, :], hT[:, h, k, c * BANK:(c + 1) * BANK],
                                        start=(i == k == 0), stop=(i == 2 and k == KT - 1))
                return last
            m = put("tensor", product, (wqk_in[P], *h_ready, *freed[bank]), "projected")
            span = slice(c * BANK, (c + 1) * BANK)
            halves = []
            for head in range(2):
                r = slice(head * DH, (head + 1) * DH)
                o = slice((1 - head) * DH, (2 - head) * DH)
                hi = qk[r, par, head, 0 if kind == 0 else 1, span]
                lo = qk[o, par, head, 0, span] if kind == 0 else qk[r, par, head, 2, span]
                scale = SCALE if kind == 0 else 1.0
                a = put("scalar", lambda e, hi=hi, r=r, scale=scale: e.activation(
                    hi, banks[bank][r, :], ACT.Copy, scale=scale),
                    (m, s_done.get(f"pair{P - 2}"), k_dup.get(P - 2), keys2_stored[0] if par else None),
                    "split_hi")
                halves.append((r, hi, lo, scale, a))
            for r, hi, lo, scale, a in halves:
                d = put("vector", lambda e, r=r, hi=hi, lo=lo, scale=scale: e.scalar_tensor_tensor(
                    lo, banks[bank][r, :], scale, hi.bitcast(F32), ALU.mult, ALU.subtract), (a,), "split_lo")
            freed[bank] = (d,)
            (q_ready if kind == 0 else k_ready)[P, c] = (a, d)
            qk_done[P] = m

        def duplicate_k(P):
            for head in range(2):
                r, o = slice(head * DH, (head + 1) * DH), slice((1 - head) * DH, (2 - head) * DH)
                t = dma(lambda e, head=head, r=r, o=o: e.dma_start(
                    qk[o, P % 2, head, 1:3, :].bitcast(F32), qk[r, P % 2, head, 1:3, :].bitcast(F32)),
                    (*k_ready[P, 0], *k_ready[P, 1]), f"k_doubled{P % 2}")
            k_dup[P] = t

        def project_v(D, u, h_ready):
            def product(e):
                for j in range(2):
                    t = 2 * u + j
                    for i, (h, w) in enumerate(TERMS):
                        for k in range(KT):
                            last = e.matmul(PJ[:, j * DIM:j * DIM + 2 * PART], hT[:, h, k, t * PART:(t + 1) * PART],
                                            wv[:, w, k, :], start=(i == k == 0), stop=(i == 2 and k == KT - 1))
                return last
            m = put("tensor", product, (wv_in[D], *h_ready, *freed["PJ"]), "projected")
            dst = v_sb[:, 2 * u:2 * u + 2, :].rearrange("p t n -> p (t n)")
            v_ready[D, u] = put("scalar", lambda e: e.copy(dst, PJ[:, 0:4 * PART]), (m, pv_part.get((D, u))), "v_copied")
            freed["PJ"] = (v_ready[D, u],)
            v_done[D] = m

        norm_done, exp_done, max_done, pT_written, o_written = {}, {}, {}, {}, {}

        def score(n):
            P, it, head = n // (2 * TILES), n // 2 % TILES, n % 2
            a = f"S{n % 2}a", f"S{n % 2}b"

            def product(e):
                q = qk[:, P % 2, head, 0, it * PART:(it + 1) * PART]
                for half in range(2):
                    for part in (1, 2):
                        last = e.matmul(SC[n % 2][:, half * BANK:(half + 1) * BANK], q,
                                        qk[:, P % 2, head, part, half * BANK:(half + 1) * BANK],
                                        start=(part == 1), stop=(part == 2))
                return last
            s_done[n] = put("tensor", product, (*q_ready[P, it * PART // BANK], *k_ready[P, 1], k_dup[P],
                                                *freed[a[0]], *freed[a[1]]), "scored")
            if it == TILES - 1 and head == 1:
                s_done[f"pair{P}"] = s_done[n]

        def row_max(n):
            max_done[n] = put("vector", lambda e: e.tensor_reduce(
                nmax[:, n % 8:n % 8 + 1], SC[n % 2][:, :], AX.X, ALU.max, negate=True), (s_done[n],), "row_max")

        def exponential(n):
            exp_done[n] = put("scalar", lambda e: e.activation(
                probs[:, n % 3, :], SC[n % 2][:, :], ACT.Exp, bias=nmax[:, n % 8:n % 8 + 1],
                accum_out=lsum[:, n % 8:n % 8 + 1]), (max_done[n], t_done.get(n - 3), probs_free[0]), "exponential")
            freed[f"S{n % 2}a"] = freed[f"S{n % 2}b"] = (exp_done[n],)

        def normalise(n):
            t = put("vector", lambda e: e.reciprocal(rsum[:, n % 8:n % 8 + 1], lsum[:, n % 8:n % 8 + 1]),
                    (exp_done[n],), "row_sum")
            norm_done[n] = put("gpsimd", lambda e: e.tensor_scalar(
                probs[:, n % 3, :], probs[:, n % 3, :], rsum[:, n % 8:n % 8 + 1], 1.0, ALU.mult, ALU.mult),
                (t, exp_done[n]), "normalised")

        def turn(n):
            g, it, head = n // 4, n // 2 % 2, n % 2
            for half in range(2):
                bank = f"T{half}"

                def product(e, half=half, bank=bank):
                    for j in range(4):
                        jt = half * 4 + j
                        last = e.transpose(banks[bank][:, j * PART:(j + 1) * PART],
                                           probs[:, n % 3, jt * PART:(jt + 1) * PART], ident[:, :])
                    return last
                t_done[n] = put("tensor", product, (norm_done[n], *freed[bank]), "turned_p")
                dst = pT[:, g % 2, head, half * 4:half * 4 + 4, it * PART:(it + 1) * PART]
                src = banks[bank].rearrange("p (j n) -> p j n", j=4)
                waits = (t_done[n], pv_part.get(("group", g - 2)))
                if half == 0:
                    t = put("scalar", lambda e, dst=dst, src=src: e.copy(dst, src), waits, "pT_act")
                else:
                    t = put("vector", lambda e, dst=dst, src=src: e.tensor_copy(dst, src), waits, "pT_dve")
                freed[bank] = (t,)
                pT_written[n, half] = t

        def attend(g, part):
            P = g * 4 // (2 * TILES)

            def product(e):
                for jt in range(part * TILES // 2, (part + 1) * TILES // 2):
                    for head in range(2):
                        r = slice(head * DH, (head + 1) * DH)
                        c0 = (P % 2) * PART + head * DH
                        last = e.matmul(PV[r, 0:2 * PART], v_sb[:, jt, c0:c0 + DH], pT[:, g % 2, head, jt, :],
                                        start=(jt == 0), stop=(jt == TILES - 1))
                return last
            waits = [v_ready[P // 2, 2 * part], v_ready[P // 2, 2 * part + 1], *freed["PV"]]
            waits += [pT_written[4 * g + i, h] for i in range(4) for h in range(2)]
            t = put("tensor", product, waits, "attended")
            pv_part[P // 2 + 1, 2 * part] = pv_part[P // 2 + 1, 2 * part + 1] = t
            if part == 1:
                pv_part["group", g] = t
                i0 = (g * 2 % TILES) * PART
                o_written[P] = put("scalar", lambda e: e.copy(oT[:, P % PAIRS, i0:i0 + 2 * PART],
                                                              PV[:, 0:2 * PART]),
                                   (t, *oT_free), "oT_written")
                freed["PV"] = (o_written[P],)

        steps = PAIRS * 2 * TILES

        def self_attention(b, h_ready, extra):
            P0, n0, W = b * PAIRS, b * steps, 2 * TILES
            for i in range(steps + 9):
                n, p, s = n0 + i, i // W, i % W
                if i == 0:
                    project_v(P0 // 2, 0, h_ready)
                    project_v(P0 // 2, 1, h_ready)
                if i < steps:
                    score(n)
                if 0 <= i - 1 < steps - 1:
                    normalise(n - 1)
                if i < steps:
                    row_max(n)
                if 0 <= i - 2 < steps:
                    turn(n - 2)
                if i < steps:
                    exponential(n)
                if i == steps - 1:
                    normalise(n)
                j = i - 6
                if 0 <= j < steps and j % 2 == 0:
                    attend((n0 + j) // 4, j % 4 // 2)
                P = P0 + p
                first_v = -2 if p == 0 else 3
                if i < steps and p % 2 == 0 and first_v <= s < first_v + 4:
                    project_v(P // 2, s - first_v, h_ready)
                if s in (7, 9, 11, 13) and p + 1 < PAIRS:
                    u = (s - 7) // 2
                    project_qk(P + 1, 1 if u < 2 else 0, u % 2, h_ready)
                    if u == 1:
                        duplicate_k(P + 1)
                if s == 8 and i < steps and p % 2 == 0 and P // 2 + 1 < B * PAIRS // 2:
                    stream_v(P // 2 + 1)
                if s == 14 and i < steps and P + 2 < B * PAIRS:
                    stream_qk(P + 2)
                extra(i)

        ring_read = {}
        bias_added = {}

        def output(b, t, ring, slot, ready, w, name, bank):
            turned = (turned1, turned2)[ring]

            def product(e):
                for i, (o, h) in enumerate(TERMS):
                    for p in range(PAIRS):
                        last = e.matmul(banks[bank][:, 0:DIM], turned[:, slot, o, p, :], w[:, h, p, :],
                                        start=(i == p == 0), stop=(i == 2 and p == PAIRS - 1))
                return last
            m = put("tensor", product, (*ready, *freed[bank]), "out_product")
            ring_read[ring, slot] = m
            added = put("vector", lambda e: e.tensor_tensor(
                xres[:, b % 2, t, :], banks[bank][:, 0:DIM], xres[:, b % 2, t, :], ALU.add),
                (m, bias_added[b, t]), name)
            freed[bank] = (added,)
            return m, added

        def add_bias(b, i, tiles, waits):
            for t in tiles:
                bias_added[b, t] = put("gpsimd", lambda e, t=t: e.tensor_tensor(
                    xres[:, b % 2, t, :], xres[:, b % 2, t, :], rows[:, i, :], ALU.add),
                    (*waits, rows_in), "bias_added")

        oT_split = {}

        def split_oT(b, t, engine="vector"):
            hi, lo = turned1[:, t % 3, 0], turned1[:, t % 3, 1]
            src = oT[:, :, t * PART:(t + 1) * PART]
            free = (s_done[f"pair{b * PAIRS + PAIRS - 2}"], ring_read.get((0, t % 3)))
            h = put("scalar", lambda e: e.copy(hi, src), (o_written[b * PAIRS + PAIRS - 1], *free), "oT_hi")
            lo_in = put(engine, lambda e: e.tensor_tensor(lo, src, hi.bitcast(F32), ALU.subtract), (h, *free),
                        f"oT_lo_{engine}")
            oT_split[t] = [h, lo_in]
            if t == TILES - 1:
                oT_free[:] = [h, lo_in, *oT_split[TILES - 2]]

        def output1(b, t, bank="PJ"):
            return output(b, t, 0, t % 3, (*oT_split[t], wo1_in), wo1, "x1_added", bank)

        def cross_attention(b, h_ready, keys_in, values_in, before_round, behind_score, extra):
            scored2, exp2, inverse2, scaled2, turned_ready, p2_read = {}, {}, {}, {}, {}, {}
            x_done = {}

            HB = HEADS // 2

            def score2(t):
                for half in range(2):
                    bank = f"S{t % 2}" + "ab"[half]

                    def product(e, half=half, bank=bank):
                        for i, (h, w) in enumerate(TERMS):
                            for k in range(KT):
                                last = e.matmul(banks[bank], hT[:, h, k, t * PART:(t + 1) * PART],
                                                keys_hl[:, w, k, half * BANK:(half + 1) * BANK],
                                                start=(i == k == 0), stop=(i == 2 and k == KT - 1))
                        return last
                    scored2[t] = put("tensor", product, (*h_ready[t // TPC], *keys_in[half], *freed[bank]), "scored2")
                hT_read[0] = scored2[t]

            def exponential2(t):
                s3 = SC[t % 2][:, :].rearrange("p (h m) -> p h m", h=HEADS)
                P3 = probs[:, t % 3, :].rearrange("p (h m) -> p h m", h=HEADS)
                nm, ls = nmax2[:, t % 2, :], lsum2[:, t % 2, :]
                mx = put("vector", lambda e: e.tensor_reduce(nm, s3, AX.X, ALU.max, negate=True),
                         (scored2[t], exp2.get(t - 2), soft2_last[0]), "soft2")
                sub = put("vector", lambda e: e.tensor_tensor(
                    P3[:, HB:], s3[:, HB:], nm[:, HB:].unsqueeze(2).to_broadcast([PART, HB, M]), ALU.add),
                    (mx, p2_read.get(t - 3)), "soft2")
                soft2_last[0] = sub
                freed[f"S{t % 2}b"] = (sub,)

                def exponentials(e):
                    for h in range(HB):
                        last = e.activation(P3[:, h], s3[:, h], ACT.Exp, bias=nm[:, h:h + 1],
                                            accum_out=ls[:, h:h + 1])
                    return last
                first = put("scalar", exponentials, (mx, p2_read.get(t - 3), inverse2.get(t - 2)), "exp2")
                freed[f"S{t % 2}a"] = (first,)
                exp2[t] = put("scalar", lambda e: e.activation(
                    probs[:, t % 3, BANK:], probs[:, t % 3, BANK:], ACT.Exp), (sub,), "exp2")

            def soften2(t):
                P3 = probs[:, t % 3, :].rearrange("p (h m) -> p h m", h=HEADS)
                ls, rr = lsum2[:, t % 2, :], rsum2[:, t % 2, :]
                su = put("vector", lambda e: e.tensor_reduce(ls[:, HB:], P3[:, HB:], AX.X, ALU.add),
                         (exp2[t], soft2_last[0]), "soft2")
                inverse2[t] = put("vector", lambda e: e.reciprocal(rr, ls), (su, scaled2.get(t - 2)), "soft2")
                soft2_last[0] = inverse2[t]
                scaled2[t] = put("gpsimd", lambda e: e.tensor_tensor(
                    P3, P3, rr.unsqueeze(2).to_broadcast([PART, HEADS, M]), ALU.mult), (inverse2[t],), "scaled2")

            def turn2(t):
                slot = t % 3
                turned_ready[t] = (slot,)
                for half in range(2):
                    bank = f"T{half}"

                    def product(e, half=half, bank=bank):
                        for j in range(4):
                            p = half * 4 + j
                            last = e.transpose(banks[bank][:, j * PART:(j + 1) * PART],
                                               probs[:, t % 3, p * PART:(p + 1) * PART], ident[:, :])
                        return last
                    m = put("tensor", product, (scaled2[t], *freed[bank]), "turned2")
                    p2_read[t] = probs_free[0] = m
                    hi, lo = (turned2[:, slot, w, half * 4:half * 4 + 4, :].rearrange("p j n -> p (j n)")
                              for w in range(2))
                    h = put("scalar", lambda e, hi=hi, bank=bank: e.copy(hi, banks[bank]),
                            (m, ring_read.get((1, slot))), "p2T_hi")
                    d = put("vector", lambda e, hi=hi, lo=lo, bank=bank: e.tensor_tensor(
                        lo, banks[bank], hi.bitcast(F32), ALU.subtract), (h, ring_read.get((1, slot))), "p2T_lo")
                    freed[bank] = (d,)
                    turned_ready[t] += (h, d)

            def out2(t):
                slot, *ready = turned_ready[t]
                out_done[0], x_done[t] = output(b, t, 1, slot, (*ready, *values_in), values_hl, "x2_added",
                                                ("PJ", "PV")[t % 2])
                ln3_done[b] = ln_stats(xres[:, b % 2, t, :], mv3[:, b, t, :], t, x_done[t])

            for i in range(TILES + 3):
                if 0 <= i - 1 < TILES:
                    soften2(i - 1)
                before_round(i)
                if i >= TILES:
                    out2(i - 3)
                if 0 <= i - 2 < TILES:
                    turn2(i - 2)
                if i < TILES:
                    score2(i)
                    behind_score(i)
                    exponential2(i)
                if 3 <= i < TILES:
                    out2(i - 3)
                extra(i)
            return x_done

        soft2_last, hT_read, out_done = [None], [None], [None]
        ln3_done = {}

        NCH = B * CHUNKS
        x_stored, rstd3, ffn_rows = {}, {}, [None]
        xf_in, biased, h3, u_ready, up_read, down_read, gate_read, u_read, stored = ({} for _ in range(9))
        wp_in = {}

        def split_ffn(q, engine="scalar"):
            n, f4 = QF // 2, FT // 4
            tickets = ()
            for raw, hi, lo in ((raw_wp[:, :, :].rearrange("p k (g n) -> p k g n", g=2)[:, :, :, q * n:(q + 1) * n],
                                 wp[q][:, 0], wp[q][:, 1]),
                                (raw_w2[:, q * f4:(q + 1) * f4], w2[:, 0, q * f4:(q + 1) * f4],
                                 w2[:, 1, q * f4:(q + 1) * f4])):
                free = out_done[0] if q == 3 else values_in_last[0]
                if engine == "gpsimd":
                    tickets += (split_weights(raw, hi, lo, ffn_raw[0], free, "ffn_split"),)
                    continue
                h = put("scalar", lambda e, hi=hi, raw=raw: e.copy(hi, raw), (ffn_raw[0], free), "ffn_hi")
                tickets += (h, put("vector", lambda e, hi=hi, lo=lo, raw=raw: e.tensor_tensor(
                    lo, raw, hi.bitcast(F32), ALU.subtract), (h,), "ffn_lo"))
            wp_in[q] = tickets

        ffn_raw, values_in_last = [None], [None]

        def load_chunk(c):
            b, t0 = c // CHUNKS, (c % CHUNKS) * TPC
            under = B - 2 + c // 2 if c < 4 else b
            xf_in[c] = dma(lambda e: e.dma_start(xf[:, c % 4], xmid[b, :, t0:t0 + TPC, :]),
                           (x_stored[b], x_stored[under], ln3_done[under], stored.get(c - 4), xf_in.get(c - 4)),
                           f"xf_loaded{c % 4}")

        def chunk_rows(c):
            b, t0 = c // CHUNKS, (c % CHUNKS) * TPC
            tiles = [(xf[:, c % 4, j, :], mv3[:, b, t0 + j, 0:1],
                      rs3[:, b, t0 + j:t0 + j + 1]) for j in range(TPC)]
            ready = ln_rows(tiles, (rstd3[b], xf_in[c]))
            biased[c] = put("gpsimd", lambda e: e.tensor_tensor(
                xf[:, c % 4], xf[:, c % 4], rows[:, 2:3, :].to_broadcast([PART, TPC, DIM]), ALU.add),
                (ready, rows_in), "bias3_added")
            return ready

        def chunk_turn(c, ready, **how):
            h3[c] = ln_turn(c % 2, ready, 2, (up_read.get(c - 2, hT_read[0]),), **how)

        def ffn_up(c, f):
            i = c * FT + f
            for which, bank in ((1, ("S0a", "S1a")[f % 2]), (0, ("S0b", "S1b")[f % 2])):
                col = which * FT + f
                q, o = f * 4 // FT, f % (FT // 4) * PART

                def product(e, which=which, bank=bank, q=q, o=o):
                    for i, (w, h) in enumerate(TERMS):
                        for k in range(KT):
                            last = e.matmul(banks[bank], wp[q][:, w, k, which, o:o + PART],
                                            hT[:, h, k, (c % 2) * BANK:(c % 2 + 1) * BANK],
                                            start=(i == k == 0), stop=(i == 2 and k == KT - 1))
                    return last
                m = put("tensor", product, (*h3[c], *wp_in[f * 4 // FT], *freed[bank]), "up_product")
                if which == 1:
                    g = put("scalar", lambda e, bank=bank, col=col: e.activation(
                        gate[:, i % 4, :], banks[bank], ACT.Gelu, bias=bp_col[:, col:col + 1]),
                        (m, bp_in, gate_read.get(i - 4)), "gelu")
                    freed[bank] = (g,)
                else:
                    u = put("vector", lambda e, bank=bank, col=col: e.scalar_tensor_tensor(
                        u_full[:, i % 3, :], banks[bank], bp_col[:, col:col + 1], gate[:, i % 4, :],
                        ALU.add, ALU.mult), (m, g, u_read.get(i - 3)), "gated")
                    freed[bank] = (u,)
                    gate_read[i] = u
            hi, lo = uT[c % 2][:, 0, f, :], uT[c % 2][:, 1, f, :]
            free = down_read.get(c - 2)
            h = put("scalar", lambda e: e.copy(hi, u_full[:, i % 3, :]), (u, free), "u_hi")
            u_read[i] = put("vector", lambda e: e.tensor_tensor(lo, u_full[:, i % 3, :], hi.bitcast(F32),
                                                                ALU.subtract), (h, free), "u_lo")
            u_ready[c] = (h, u_read[i])
            up_read[c] = m

        def ffn_down(c, j):
            b, t0 = c // CHUNKS, (c % CHUNKS) * TPC
            bank = ("PV", "PJ")[j % 2]

            def product(e):
                for i, (o, h) in enumerate(TERMS):
                    for f in range(FT):
                        last = e.matmul(banks[bank][:, 0:DIM], uT[c % 2][:, o, f, j * PART:(j + 1) * PART],
                                        w2[:, h, f, :], start=(i == f == 0), stop=(i == 2 and f == FT - 1))
                return last
            m = put("tensor", product, (*u_ready[c], *wp_in[3], *freed[bank]), "down_product")
            down_read[c] = m
            y = put("vector", lambda e: e.tensor_tensor(xf[:, c % 4, j, :], banks[bank][:, 0:DIM],
                                                        xf[:, c % 4, j, :], ALU.add), (m, biased[c]), "y_added")
            freed[bank] = (y,)
            if j == TPC - 1:
                dst = out[b, t0 * PART:(t0 + TPC) * PART, :].rearrange("(t p) d -> p t d", p=PART)
                stored[c] = dma(lambda e: e.dma_start(dst, xf[:, c % 4]), (y,), f"y_stored{c % 2}")

        h1_ready = {}

        def stats1(b, t):
            agg1[0] = ln_stats(xres[:, b % 2, t, :], mv1[:, t, :], t, x_in[b])

        def rstd_1(b):
            rstd1[b] = ln_rstd(mv1[:, :, 1], rs1[:, :], (agg1[0],))

        agg1, rstd1 = [None], {}

        ln1 = {}

        def norm1(b, c, engine="vector"):
            ln1[c] = ln_rows(rows_of(b, c, mv1, rs1), (rstd1[b],), engine)
            add_bias(b, 0, range(c * TPC, (c + 1) * TPC), (ln1[c],))

        def turn_norm1(b, c, **how):
            h1_ready[b, c] = ln_turn(c, ln1[c], 0, (hT_read[0],), **how)

        def first_qk(b, u):
            h = [t for c in range(CHUNKS) for t in h1_ready[b, c]] if u % 2 else h1_ready[b, 0]
            project_qk(b * PAIRS, 1 if u < 2 else 0, u % 2, h, ("S0a", "S0b", "S1a", "S1b")[u])
            if u == 1:
                duplicate_k(b * PAIRS)

        for t in range(TILES):
            stats1(0, t)
        rstd_1(0)
        context_turn()
        for c in range(CHUNKS):
            norm1(0, c)
            turn_norm1(0, c)
            context_product(c)
        for u in range(4):
            first_qk(0, u)
        values2_stored = context_fold()
        oT_free[:] = [values2_stored]
        probs_free[0] = keys2_stored[0]
        for b in range(B):
            P0 = b * PAIRS
            last = b == B - 1
            h_all = [t for c in range(CHUNKS) for t in h1_ready[b, c]]
            if not last:
                x_in[b + 1] = load_x(b + 1, (x_stored.get(b - 1, wo1_in), ln3_done.get(b - 1)))
            x1, ln2, h2_ready, r2, split_in = {}, {}, {}, {}, {}

            def raw_cross_load(i, free, b=b):
                raw = (raw_keys2, raw_values2)[i]
                return dma(lambda e: e.dma_start(raw[:, :], cross_dram[b, :, i]),
                           ((keys2_stored[0], values2_stored)[i], *free), f"raw_cross{i}_loaded")

            def split_cross(i, part, raw_in, group_over, engine="vector"):
                raw = (raw_keys2, raw_values2)[i]

                def view(x):
                    x = x.rearrange("p (k h n) -> p k h n", k=KT, h=2)[:, :, part] if i == 0 else \
                        x.rearrange("p (h n) -> p h n", h=2)[:, part]
                    return x
                hi, lo, src = view(cross[:, i, 0]), view(cross[:, i, 1]), view(raw[:, :])
                h = put("scalar", lambda e: e.copy(hi, src), (raw_in, group_over), "cross_hi")
                return h, put(engine, lambda e: e.tensor_tensor(lo, src, hi.bitcast(F32), ALU.subtract), (h,),
                              f"cross_lo_{engine}")

            def out1(t, bank="PJ", b=b, x1=x1):
                x1[t] = output1(b, t, bank)[1]
                x1["agg"] = ln_stats(xres[:, b % 2, t, :], mv2[:, t, :], t, x1[t])

            def rstd_2(c, b=b, x1=x1, r2=r2):
                sl = slice(c * TPC, (c + 1) * TPC)
                r2[c] = ln_rstd(mv2[:, sl, 1], rs2[:, sl], (x1["agg"],))

            def norm2(c, engine="vector", b=b, ln2=ln2, r2=r2):
                ln2[c] = ln_rows(rows_of(b, c, mv2, rs2), (r2[c],), engine)

            def bias2(c, part, b=b, ln2=ln2):
                t0 = c * TPC + part * TPC // 2
                add_bias(b, 1, range(t0, t0 + TPC // 2), (ln2[c],))

            def turn_norm2(c, P0=P0, ln2=ln2, h2_ready=h2_ready, **how):
                h2_ready[c] = ln_turn(c, ln2[c], 1, (qk_done[P0 + PAIRS - 1], v_done[(P0 + PAIRS - 1) // 2]), **how)

            keys_in = {}

            def beside_attention(i, b=b, last=last, keys_in=keys_in):
                if not last and i >= steps // 2 and i % 4 == 0 and (i - steps // 2) // 4 < TILES:
                    stats1(b + 1, (i - steps // 2) // 4)
                j = i - (steps - 2 * TILES + 8)
                if j == 9:
                    keys_in["raw"] = raw_cross_load(0, (t_done[(b + 1) * steps - 1],))
                if j == 10:
                    norm2(0)
                if j in (0, 2, 4, 6, 8, 10):
                    split_oT(b, j // 2)
                if j in (3, 5, 7, 9, 11, 13):
                    out1((j - 3) // 2)
                if j == 11:
                    turn_norm2(0)
                if j == 9:
                    rstd_2(0)
                    if not last:
                        rstd_1(b + 1)
                    if b:
                        rstd_3(b - 1)
                if j in (12, 13):
                    keys_in[j - 12] = split_cross(0, j - 12, keys_in["raw"],
                                                  pv_part["group", (b + 1) * steps // 4 - 2])

            def rstd_3(b):
                rstd3[b] = ln_rstd(mv3[:, b, :, 1], rs3[:, b, :], (ln3_done[b],))

            self_attention(b, h_all, beside_attention)
            group_over = pv_part["group", (b + 1) * steps // 4 - 1]
            raw_values = raw_cross_load(1, (group_over,))
            split_oT(b, 6)
            split_oT(b, 7, "gpsimd")
            values_in = [t for part in range(2) for t in split_cross(1, part, raw_values, group_over, "gpsimd")]
            values_in_last[0] = values_in[-1]
            if last:
                dma(lambda e: e.dma_start(raw_wp[:, :, :], Wp.rearrange("(k p) n -> p k n", p=PART)),
                    tuple(oT_free), "ffn_loaded")
                ffn_raw[0] = dma(lambda e: e.dma_start(raw_w2[:, :, :], W2.rearrange("(f p) n -> p f n", p=PART)),
                              tuple(oT_free), "ffn_loaded")
                for c in range(2):
                    load_chunk(c)

            later = {}

            def beside_cross(i, b=b, last=last, later=later, x1=x1, r2=r2,
                             h2_ready=h2_ready):
                if i == 0:
                    out1(6, "PV")
                if i == 1:
                    r2[1] = ln_inverse(rs2[:, TPC:], later["root2"])
                    norm2(1)
                if i == 2:
                    h2_ready[1] = h2_ready[1]()
                if i in (1, 2, 3, 4):
                    bias2((i - 1) // 2, (i - 1) % 2)
                if last:
                    if i in (4, 6):
                        split_ffn((i - 4) // 2, "gpsimd")
                    if i == 5:
                        ffn_rows[0] = chunk_rows(0)
                elif 3 <= i < 3 + TPC:
                    ln1[0] = ln_rows(rows_of(b + 1, 0, mv1, rs1), (rstd1[b + 1],), slots=(i - 3,))
                elif i == 3 + TPC:
                    add_bias(b + 1, 0, range(TPC), (ln1[0],))
                if i == TILES - 1:
                    if last:
                        h3[0] = h3[0]()
                    else:
                        h1_ready[b + 1, 0] = h1_ready[b + 1, 0]()
                        norm1(b + 1, 1)
                if not last:
                    if i == TILES:
                        first_qk(b + 1, 0)
                        first_qk(b + 1, 2)
                    if i == TILES + 1:
                        first_qk(b + 1, 1)
                        first_qk(b + 1, 3)

            def before_round(i, b=b, last=last, later=later, x1=x1):
                if i == 1:
                    out1(7)
                    later["root2"] = ln_root(mv2[:, TPC:, 1], (x1["agg"],))
                if i == TILES + 1 and not last:
                    turn_norm1(b + 1, 1, through=("S1b", "S0b"))

            def behind_score(i, b=b, last=last, turn_norm2=turn_norm2):
                if i == 2:
                    turn_norm2(1, through=("PJ", "PV"), defer=True)
                if i == TILES - 1 and last:
                    chunk_turn(0, ffn_rows[0], through=("S0a", "S0b"), defer=True)
                elif i == TILES - 1:
                    turn_norm1(b + 1, 0, through=("S0a", "S0b"), defer=True)

            cross_attention(b, h2_ready, keys_in, values_in, before_round, behind_score, beside_cross)
            x_stored[b] = dma(lambda e, b=b: e.dma_start(xmid[b], xres[:, b % 2]), (ln3_done[b],),
                              f"x_stored{b % 2}")

        rstd_3(B - 1)
        for c in range(2, 4):
            load_chunk(c)
        for c in range(NCH + 1):
            for f in range(FT):
                if c < NCH:
                    ffn_up(c, f)
                    if c == 0 and f in (0, 2):
                        split_ffn(f // 2 + 2)
                if f == 3 and c + 1 < NCH:
                    rows_ready = chunk_rows(c + 1)
                if f == 5 and c + 1 < NCH:
                    chunk_turn(c + 1, rows_ready)
                if c and f % 2 == 1:
                    ffn_down(c - 1, f // 2)
            if c and c + 3 < NCH:
                load_chunk(c + 3)

        block = stack.enter_context(nc.Block())

        @block.tensor
        def _(e):
            Q.play("tensor", e)

        @block.vector
        def _(e):
            Q.play("vector", e)

        @block.scalar
        def _(e):
            Q.play("scalar", e)

        @block.gpsimd
        def _(e):
            Q.play("gpsimd", e)

        @block.sync
        def _(e):
            Q.play("sync", e)
            for name in ("keys2_stored", "values2_stored", "x_stored0", "x_stored1", "y_stored0", "y_stored1"):
                e.wait_ge(semaphore(name), Q.raised[name])


_NAMES = ["x", "ctx_768"] + ["L0_xattn_" + n for n in (
    "Wq1 Wk1 Wv1 Wo1 bo1 Wq2 Wk2 Wv2 Wo2 bo2 Wp bp W2 b2 g1 be1 g2 be2 g3 be3").split()]


def kernel(**inputs):
    import numpy as np
    import concourse.bacc as bacc
    from concourse import mybir as mb
    from concourse.bass_utils import run_bass_kernel_spmd

    nc = bacc.Bacc("TRN2", target_bir_lowering=False, num_devices=1)
    arrays, args = {}, []
    for name in _NAMES:
        a = np.ascontiguousarray(inputs[name])
        arrays[f"in_{name}"] = a
        args.append(nc.dram_tensor(f"in_{name}", a.shape, mb.dt.from_np(a.dtype), kind="ExternalInput").ap())
    shape = inputs["x"].shape
    args.append(nc.dram_tensor("out_x", shape, mb.dt.float32, kind="ExternalOutput").ap())
    block_kernel(nc, *args)
    r = run_bass_kernel_spmd(nc, [arrays], core_ids=[0])
    return r.results[0]["out_x"]
```
